# Optimizing a Trainium2 kernel written in Bass

```python
import numpy as np
import jax
import jax.numpy as jnp

def _softmax(x, axis=-1):
    return jax.nn.softmax(x, axis=axis)

def _gelu(x):
    return jax.nn.gelu(x, approximate=True)

def _silu(x):
    return jax.nn.silu(x)

def _sigmoid(x):
    return jax.nn.sigmoid(x)

def _layernorm(x, axis=-1, eps=1e-05):
    m = jnp.mean(x, axis=axis, keepdims=True)
    v = jnp.var(x, axis=axis, keepdims=True)
    return (x - m) / jnp.sqrt(v + eps)

def _scatter_add(tgt, idx, src, axis=0):
    return tgt.at[idx].add(src)

def _segment_sum(src, seg, n):
    return jax.ops.segment_sum(src, seg, n)
kernel_name = 'mk_gnn_resnorm_d2_gnn_r64_49bef8'

def setup_inputs(seed: int=0):
    np.random.seed(seed)
    _w = jnp.asarray

    def _rec_inputs():
        import jax
        import jax.numpy as jnp
        _gk = jax.random.key(seed)
        x = -0.0003713 + 1 * jax.random.normal(jax.random.fold_in(_gk, 1), (50000, 128), jnp.float32)
        src = jax.random.randint(jax.random.fold_in(_gk, 2), (12500,), 0, 50000, jnp.int32)
        dst = jax.random.randint(jax.random.fold_in(_gk, 3), (12500,), 0, 50000, jnp.int32)
        _o = jnp.argsort(dst, stable=True)
        src = src[_o]
        dst = dst[_o]
        return (x, src, dst)
    x, src, dst = _rec_inputs()

    def _L0_gnn_setup():
        import jax, jax.numpy as jnp
        import numpy as np
        N, E, D = (100000, 500000, 128)
        key = jax.random.key(seed)
        ks = jax.random.split(key, 8)
        s = 1.0 / np.sqrt(D)
        return {'node_feat': jax.random.normal(ks[0], (N, D), dtype=jnp.float32), 'edge_index': jax.random.randint(ks[1], (2, E), 0, N, dtype=jnp.int64), 'W_edge': jax.random.normal(ks[2], (2 * D, D), dtype=jnp.float32) * s, 'b_edge': jnp.zeros((D,), dtype=jnp.float32), 'W1': jax.random.normal(ks[3], (D, D), dtype=jnp.float32) * s, 'b1': jnp.zeros((D,), dtype=jnp.float32), 'W2': jax.random.normal(ks[4], (D, D), dtype=jnp.float32) * s, 'b2': jnp.zeros((D,), dtype=jnp.float32), 'eps': jnp.zeros((1,), dtype=jnp.float32)}
    _L0_gnn_all = _L0_gnn_setup()
    _L0_gnn_in = {k: v for k, v in _L0_gnn_all.items() if k in ('W_edge', 'b_edge', 'W1', 'b1', 'W2', 'b2', 'eps')}
    del _L0_gnn_all

    def _L1_gnn_setup():
        import jax, jax.numpy as jnp
        import numpy as np
        N_NODES = 100000
        N_EDGES = 25000
        D_IN = 128
        P = 128

        def graph_conv(feat, W, b, src, dst, n_nodes):
            ones = jnp.ones((src.shape[0],), dtype=feat.dtype)
            deg_out = jnp.clip(jax.ops.segment_sum(ones, src, num_segments=n_nodes), 1.0)
            deg_in = jnp.clip(jax.ops.segment_sum(ones, dst, num_segments=n_nodes), 1.0)
            h = feat * (deg_out ** (-0.5))[:, None]
            h = h @ W
            agg = jax.ops.segment_sum(h[src], dst, num_segments=n_nodes)
            return agg * (deg_in ** (-0.5))[:, None] + b
        key = jax.random.key(seed)
        k = jax.random.split(key, 10)
        features = jax.random.normal(k[0], (N_NODES, D_IN), dtype=jnp.float32)
        src = jax.random.randint(k[1], (N_EDGES,), 0, N_NODES, dtype=jnp.int32)
        dst = jax.random.randint(k[2], (N_EDGES,), 0, N_NODES, dtype=jnp.int32)
        s1 = 1.0 / np.sqrt(D_IN)
        s2 = 1.0 / np.sqrt(P)
        W1 = jax.random.normal(k[3], (D_IN, P), dtype=jnp.float32) * s1
        b1 = jnp.zeros((P,), dtype=jnp.float32)
        W2 = jax.random.normal(k[4], (P, P), dtype=jnp.float32) * s2
        b2 = jnp.zeros((P,), dtype=jnp.float32)
        W3 = jax.random.normal(k[5], (P, P), dtype=jnp.float32) * s2
        b3 = jnp.zeros((P,), dtype=jnp.float32)
        return {'features': features, 'src': src, 'dst': dst, 'W1': W1, 'b1': b1, 'W2': W2, 'b2': b2, 'W3': W3, 'b3': b3}
    _L1_gnn_all = _L1_gnn_setup()
    _L1_gnn_in = {k: v for k, v in _L1_gnn_all.items() if k in ('W1', 'b1', 'W2', 'b2', 'W3', 'b3')}
    del _L1_gnn_all
    return {'x': x, 'src': src, 'dst': dst, 'L0_gnn_W_edge': _L0_gnn_in['W_edge'], 'L0_gnn_b_edge': _L0_gnn_in['b_edge'], 'L0_gnn_W1': _L0_gnn_in['W1'], 'L0_gnn_b1': _L0_gnn_in['b1'], 'L0_gnn_W2': _L0_gnn_in['W2'], 'L0_gnn_b2': _L0_gnn_in['b2'], 'L0_gnn_eps': _L0_gnn_in['eps'], 'L1_gnn_W1': _L1_gnn_in['W1'], 'L1_gnn_b1': _L1_gnn_in['b1'], 'L1_gnn_W2': _L1_gnn_in['W2'], 'L1_gnn_b2': _L1_gnn_in['b2'], 'L1_gnn_W3': _L1_gnn_in['W3'], 'L1_gnn_b3': _L1_gnn_in['b3']}

def reference(x, src, dst, L0_gnn_W_edge, L0_gnn_b_edge, L0_gnn_W1, L0_gnn_b1, L0_gnn_W2, L0_gnn_b2, L0_gnn_eps, L1_gnn_W1, L1_gnn_b1, L1_gnn_W2, L1_gnn_b2, L1_gnn_W3, L1_gnn_b3):
    import jax
    import jax.numpy as jnp

    def _L0_gnn_ref(node_feat, edge_index, W_edge, b_edge, W1, b1, W2, b2, eps):
        import jax, jax.numpy as jnp
        import numpy as np
        N, E, D = (100000, 500000, 128)
        n_nodes = node_feat.shape[0]
        src, dst = (edge_index[0], edge_index[1])
        h_src = node_feat[src]
        h_dst = node_feat[dst]
        edge_emb = jnp.concatenate([h_src, h_dst], axis=1)
        m = jax.nn.relu(edge_emb @ W_edge + b_edge)
        neigh = jax.ops.segment_sum(m, dst, num_segments=n_nodes)
        rst = (1.0 + eps[0]) * node_feat + neigh
        out = jax.nn.relu(rst @ W1 + b1) @ W2 + b2
        return out

    def _L1_gnn_ref(features, src, dst, W1, b1, W2, b2, W3, b3):
        import jax, jax.numpy as jnp
        import numpy as np
        N_NODES = 100000
        N_EDGES = 25000
        D_IN = 128
        P = 128

        def graph_conv(feat, W, b, src, dst, n_nodes):
            ones = jnp.ones((src.shape[0],), dtype=feat.dtype)
            deg_out = jnp.clip(jax.ops.segment_sum(ones, src, num_segments=n_nodes), 1.0)
            deg_in = jnp.clip(jax.ops.segment_sum(ones, dst, num_segments=n_nodes), 1.0)
            h = feat * (deg_out ** (-0.5))[:, None]
            h = h @ W
            agg = jax.ops.segment_sum(h[src], dst, num_segments=n_nodes)
            return agg * (deg_in ** (-0.5))[:, None] + b
        n = features.shape[0]
        x = jax.nn.relu(graph_conv(features, W1, b1, src, dst, n))
        x = jax.nn.relu(graph_conv(x, W2, b2, src, dst, n))
        x = jax.nn.relu(graph_conv(x, W3, b3, src, dst, n))
        return x
    edge_index = jnp.stack([src, dst])
    x = _layernorm(x + _L0_gnn_ref(x, edge_index, L0_gnn_W_edge, L0_gnn_b_edge, L0_gnn_W1, L0_gnn_b1, L0_gnn_W2, L0_gnn_b2, L0_gnn_eps), axis=-1)
    x = _layernorm(x + _L1_gnn_ref(x, src, dst, L1_gnn_W1, L1_gnn_b1, L1_gnn_W2, L1_gnn_b2, L1_gnn_W3, L1_gnn_b3), axis=-1)
    return x

_drawn_inputs = setup_inputs


def setup_inputs(seed=0):
    import zlib

    import numpy as np

    out = dict(_drawn_inputs(seed))
    spreads = {'L0_gnn_b_edge': (0.0, 0.449),
     'L0_gnn_b1': (0.0, 0.1),
     'L0_gnn_b2': (0.0, 0.1),
     'L1_gnn_b1': (0.0, 0.8),
     'L1_gnn_b2': (0.0, 0.375),
     'L1_gnn_b3': (0.0, 0.1)}
    factors = {'L1_gnn_W1': 3.009}
    for name, (base, spread) in spreads.items():
        noise = np.random.default_rng([zlib.crc32(name.encode()), seed]).standard_normal(out[name].shape)
        drawn = base * np.exp(spread * noise) if base else spread * noise
        out[name] = jnp.asarray(drawn.astype(out[name].dtype))
    for name, factor in factors.items():
        out[name] = (out[name] * factor).astype(out[name].dtype)
    return out
```

```python
import concourse.bass as bass
from concourse import mybir
from contextlib import ExitStack

N = 50000
E = 12500
D = 128
P = 128
T = -(-E // P)
EP = T * P
BODY = 14
TURNS = T // BODY
CH = BODY * P
FULL = E // P
HI, LO = 2 * T, 256
SRC_PAD = HI * LO - 1
DST_PAD, DST_END = 65535, 70000
G = 512
R = G // P
SPREAD = {"edge": 5, "conv1": 4, "conv2": 4}
LOOPED = TURNS * sum(SPREAD.values())
AHEAD = N // G - LOOPED
TAIL = N - (N // G) * G
TP = TAIL // 3
RING = 7
SLOTS = 5
STORES = 4
EPS = 1e-5


def build(nc, x, src, dst, W_edge, b_edge, W1, b1, W2, b2, eps, C1, c1, C2, c2, C3, c3, out):
    f32, bf16, i32 = mybir.dt.float32, mybir.dt.bfloat16, mybir.dt.int32
    ALU, ACT, AX = mybir.AluOpType, mybir.ActivationFunctionType, mybir.AxisListType
    ds = bass.ds
    ctx = ExitStack()
    with ctx:
        ctx.enter_context(nc.allow_non_contiguous_dma(reason="columns of biases and of edge ids, once"))

        def sb(name, shape, dt=f32):
            return ctx.enter_context(nc.sbuf_tensor(name, shape, dt))

        def sem(name):
            return ctx.enter_context(nc.semaphore(name))

        count_dram = nc.dram_tensor("count_dram", [HI * LO, 1], f32, kind="Internal").ap()
        ids_dram = nc.dram_tensor("ids_dram", [2, EP + 2], f32, kind="Internal").ap()
        y_dram = nc.dram_tensor("y_dram", [EP * 2, D], f32, kind="Internal").ap()
        u_dram = [nc.dram_tensor(f"u{n}_dram", [EP + 1, D], f32, kind="Internal").ap() for n in (1, 2)]

        same = sb("same", [P, EP])
        cont = sb("cont", [P, EP], bf16)
        above = sb("above", [T, CH], bf16)
        rows_i = sb("rows_i", [T, 2, P], i32)
        rows = sb("rows", [T, 4, P])
        tmp_i = sb("tmp_i", [T, P], i32)
        cols = sb("cols", [P, 5, T])
        srt = sb("srt", [T, 2, P + 2])
        srt_i = sb("srt_i", [T, P + 2], i32)
        before = sb("before", [T, 1])
        step_lo = sb("step_lo", [T, P + 2], bf16)
        step_hi = sb("step_hi", [T, P + 2], bf16)
        first_bc = sb("first_bc", [P, T])
        runs = sb("runs", [T, T])
        own = sb("own", [P, T])
        ends = sb("ends", [T, P])
        deg = sb("deg", [P, T])
        deg_out = sb("deg_out", [P, T])
        below = sb("below", [P, T])
        equal = sb("equal", [P, T])
        hit = sb("hit", [P, T])
        fidx = sb("fidx", [P, 2, T])
        idx = sb("idx", [P, 5, T], i32)
        SRC_I, DST_I, Y_I, U_I, O_I = range(5)
        stage = sb("stage", [P, 2, BODY], i32)
        ostage = sb("ostage", [P, BODY], i32)
        enum_i = sb("enum_i", [P, T], i32)
        enum = sb("enum", [P, T])
        ramp_i = sb("ramp_i", [P, LO], i32)
        ramp = sb("ramp", [P, LO], bf16)
        part_i = sb("part_i", [P, 1], i32)
        part = sb("part", [P, 2])
        ident = sb("ident", [P, P])
        last_row = sb("last_row", [P, P])
        hot_hi = sb("hot_hi", [P, 2, HI], bf16)
        hot_lo = sb("hot_lo", [P, 2, LO], bf16)
        tab = sb("tab", [T, 2 * LO])
        zeros = sb("zeros", [P, 512], bf16)
        junk2 = sb("junk2", [P, 2, 2, P + 1])
        ones96 = sb("ones96", [96, P], bf16)
        braw = sb("braw", [96, 2, D])
        bres = sb("bres", [96, 2, D])
        bhalf = sb("bhalf", [96, 2, D], bf16)
        bsplit = sb("bsplit", [96, 5, D], bf16)
        Wa, Wb, W1s, W2s = sb("Wa", [D, D]), sb("Wb", [D, D]), sb("W1s", [D, D]), sb("W2s", [D, D])
        Cs = [sb(f"C{n}s", [D, D]) for n in (1, 2, 3)]
        b1c = sb("b1c", [D, 1])
        eps1 = sb("eps1", [P, 1])
        epsc = sb("epsc", [P, 1])
        cb = sb("cb", [P, 3, D])
        relu_cb = sb("relu_cb", [P, 3, D])
        gx = sb("gx", [P, BODY, 2, D])
        gz = sb("gz", [P, BODY, D])
        yd = sb("yd", [P, BODY, D])
        deg_in_flight = sb("deg_in_flight", [P, BODY])
        xT = sb("xT", [P, RING, 2 * P])
        msg = sb("msg", [P, 2, D])
        aggT = sb("aggT", [P, 2, P])
        rT = sb("rT", [P, RING, 2 * P])
        hT = sb("hT", [P, 2, 2 * P])
        res = sb("res", [P, 2, 2, D])
        st = sb("st", [P, 2, 2, 6])
        mv = sb("mv", [P, 2, 2, 2])
        sd = sb("sd", [P, 2, 2])
        rs = sb("rs", [P, 2, 2])
        shift = sb("shift", [P, 2, 2])
        yo = sb("yo", [P, STORES, 2, D])
        pre = sb("pre", [P, 2, D])
        uo = sb("uo", [P, STORES, D])
        xin = sb("xin", [P, SLOTS, R * D])
        zout = sb("zout", [P, SLOTS, R * D])
        dst_bc = zout[:, :, :].rearrange("p s f -> p (s f)")[:, 0:CH]
        src_bc = xin[:, :, :].rearrange("p s f -> p (s f)")[0:T, 0:CH]
        drT = sb("drT", [P, G])
        dhT = sb("dhT", [P, G])
        dres = sb("dres", [P, R * D])
        dst1 = sb("dst1", [P, R, 6])
        dshift = sb("dshift", [P, R])
        dmv = sb("dmv", [P, R, 2])
        dsd = sb("dsd", [P, R])
        drs = sb("drs", [P, R])
        dy = sb("dy", [P, R * D])
        dst2 = sb("dst2", [P, R, 6])
        dmv2 = sb("dmv2", [P, R, 2])
        dsd2 = sb("dsd2", [P, R])
        drs2 = sb("drs2", [P, R])

        bank = [ctx.enter_context(nc.psum_tensor(f"bank{n}", [P, 512], f32)) for n in range(8)]
        pX, pM, pS, pH, pO, dX, dH, dO = bank

        s_w = sem("s_w")
        s_rows = sem("s_rows")
        s_iota = sem("s_iota")
        s_padded = sem("s_padded")
        s_v = sem("s_v")
        s_ids = sem("s_ids")
        s_pad = sem("s_pad")
        s_srt = sem("s_srt")
        s_pe = sem("s_pe")
        s_hot = sem("s_hot")
        s_hist = sem("s_hist")
        s_bc = sem("s_bc")
        s_bcused = sem("s_bcused")
        s_hi = sem("s_hi")
        s_table = sem("s_table")
        s_look = sem("s_look")
        s_looked = sem("s_looked")
        s_root = sem("s_root")
        s_ci = sem("s_ci")
        s_const_u = sem("s_const_u")
        s_held = sem("s_held")
        PHASES = ["edge", "conv1", "conv2", "conv3"]
        HALF = BODY // 2
        gat = [sem(f"gat_{k}") for k in range(BODY)]
        stored = [sem(f"stored_{k}") for k in range(STORES)]
        yd_in = [sem(f"yd_in_{h}") for h in range(2)]
        d_in = [sem(f"d_in_{k}") for k in range(SLOTS)]
        d_out = [sem(f"d_out_{k}") for k in range(SLOTS)]
        ev = {}

        def S(name):
            if name not in ev:
                ev[name] = sem(name)
            return ev[name]

        def wait(eng, semaphore, value):
            if not isinstance(value, int) or value > 0:
                eng.wait_ge(semaphore, value)

        def take_waits(eng):
            eng.sem_inc(s_held, 1)

        def step(i, k):
            return i * BODY + k

        def gathered(phase, i):
            if phase == "edge":
                return i * 48 + 48
            before = TURNS * (48 + 16 * (int(phase[4]) - 1))
            return i * 32 + (before + 16) if phase == "conv3" else i * 16 + (before + 16)

        def turns(k, slots=BODY):
            return len(range(k, BODY, slots))

        def stored_before(phase, i, k):
            slot = k % STORES
            return i * (16 * turns(slot, STORES)) + 16 * (k // STORES + PHASES.index(phase) * TURNS * turns(slot, STORES))

        def all_stored(eng, phase):
            for slot in range(STORES):
                eng.wait_ge(stored[slot], 16 * turns(slot, STORES) * TURNS * (PHASES.index(phase) + 1))

        def half_sem(name, k):
            return S(f"{name}_{k // HALF}")

        def wait_tile(eng, name, i, k):
            if k < 0:
                wait(eng, half_sem(name, BODY - 1), i * HALF)
            else:
                wait(eng, half_sem(name, k), i * HALF + (k % HALF + 1))

        class Group:
            def __init__(self, n, slot, uses, rows_, parts, start):
                self.n, self.slot, self.uses, self.r, self.p, self.start = n, slot, uses, rows_, parts, start

            def dram(self, a):
                return a[ds(self.start, self.r * self.p), :].rearrange("(p k) d -> p (k d)", k=self.r)

        def ahead_group(m):
            if m == AHEAD:
                return Group(m, m % SLOTS, m // SLOTS, 3, TP, (N // G) * G)
            return Group(m, m % SLOTS, m // SLOTS, R, P, m * G)

        def turns_of_slot(phases, j):
            return TURNS * sum(j < SPREAD[q] for q in phases)

        def looped_group(phase, i, j):
            earlier = PHASES[:PHASES.index(phase)]
            groups = TURNS * sum(SPREAD[q] for q in earlier)
            uses = len(range(j, AHEAD + 1, SLOTS)) + turns_of_slot(earlier, j)
            return Group(i * SPREAD[phase] + (groups + AHEAD + 1 + j), j, i + uses, R, P,
                         i * (SPREAD[phase] * G) + (AHEAD + groups + j) * G)

        DENSE = {"load": 0, "T": 3, "H": 4, "O": 5, "norm1": 6, "norm2": 7, "norm3": 8, "store": 9}

        def dense_pe(pe, g, stg):
            w, r = g.p, g.r
            if stg == "T":
                pe.wait_ge(d_in[g.slot], g.uses * 16 + 16)
                wait(pe, S("d_xT_out"), g.n)
                for k in range(r):
                    last = nc.tensor.transpose(dX[:, k * w:(k + 1) * w], xin[0:w, g.slot, k * D:(k + 1) * D],
                                               ident[0:w, 0:w])
                last.then_inc(S("d_xT"), 1)
            if stg == "H":
                pe.wait_ge(S("d_xT_out"), g.n + 1)
                wait(pe, S("d_h_out"), g.n)
                nc.tensor.matmul(dH[:, 0:r * w], W1s[:, :], drT[:, 0:r * w], start=True, stop=True
                                 ).then_inc(S("d_h"), 1)
            if stg == "O":
                pe.wait_ge(S("d_h_out"), g.n + 1)
                wait(pe, S("d_o_out"), g.n)
                nc.tensor.matmul(dO[0:w, 0:r * D], ones96[:, 0:w], bsplit[:, 1:1 + r, :].rearrange("p a d -> p (a d)"),
                                 start=True, stop=False)
                for k in range(r):
                    last = nc.tensor.matmul(dO[0:w, k * D:(k + 1) * D], dhT[:, k * w:(k + 1) * w], W2s[:, :],
                                            start=False, stop=(k == r - 1))
                last.then_inc(S("d_o"), 1)

        def dense_act(act, g, stg):
            w, r = g.p, g.r
            if stg == "T":
                act.wait_ge(S("d_xT"), g.n + 1)
                wait(act, S("d_h"), g.n)
                nc.scalar.activation(drT[:, 0:r * w], dX[:, 0:r * w], ACT.Identity, scale=eps1[:, 0:1]
                                     ).then_inc(S("d_xT_out"), 1)
            if stg == "H":
                act.wait_ge(S("d_h"), g.n + 1)
                wait(act, S("d_o"), g.n)
                nc.scalar.activation(dhT[:, 0:r * w], dH[:, 0:r * w], ACT.Relu, bias=b1c[:, 0:1]
                                     ).then_inc(S("d_h_out"), 1)
            if stg == "norm1":
                act.wait_ge(S("d_var1"), g.n + 1)
                nc.scalar.activation(dsd[0:w, 0:r], dmv[0:w, 0:r, 1], ACT.Sqrt, bias=epsc[0:w, 0:1]
                                     ).then_inc(S("d_sd1"), 1)
            if stg == "norm2":
                act.wait_ge(S("d_var2"), g.n + 1)
                nc.scalar.activation(dsd2[0:w, 0:r], dmv2[0:w, 0:r, 1], ACT.Sqrt, bias=epsc[0:w, 0:1]
                                     ).then_inc(S("d_sd2"), 1)
            if stg == "norm3":
                act.wait_ge(S("d_shift"), g.n + 1)
                wait(act, d_out[g.slot], g.uses * 16)
                for k in range(r):
                    last = nc.scalar.activation(zout[0:w, g.slot, k * D:(k + 1) * D], dy[0:w, k * D:(k + 1) * D],
                                                ACT.Identity, scale=drs2[0:w, k:k + 1], bias=dshift[0:w, k:k + 1])
                last.then_inc(S("d_z"), 1)

        def dense_dve(dve, g, stg):
            w, r = g.p, g.r
            if stg == "norm1":
                dve.wait_ge(S("d_o"), g.n + 1)
                nc.vector.tensor_tensor(dres[0:w, 0:r * D], dO[0:w, 0:r * D], xin[0:w, g.slot, 0:r * D], ALU.add
                                        ).then_inc(S("d_o_out"), 1)
                dve.wait_ge(S("d_o_out"), g.n + 1)
                for k in range(r):
                    last = nc.vector.bn_stats(dst1[0:w, k, :], dres[0:w, k * D:(k + 1) * D])
                last.then_inc(S("d_st1"), 1)
                dve.wait_ge(S("d_st1"), g.n + 1)
                take_waits(dve)
                for k in range(r):
                    last = nc.vector.bn_aggr(dmv[0:w, k, :], dst1[0:w, k, :])
                last.then_inc(S("d_var1"), 1)
            if stg == "norm2":
                dve.wait_ge(S("d_sd1"), g.n + 1)
                nc.vector.reciprocal(drs[0:w, 0:r], dsd[0:w, 0:r]).then_inc(S("d_rs1"), 1)
                dve.wait_ge(S("d_rs1"), g.n + 1)
                wait(dve, S("d_z"), g.n)
                for k in range(r):
                    last = nc.vector.scalar_tensor_tensor(dy[0:w, k * D:(k + 1) * D], dres[0:w, k * D:(k + 1) * D],
                                                          drs[0:w, k:k + 1], relu_cb[0:w, 2, :], ALU.mult, ALU.add)
                last.then_inc(S("d_y"), 1)
                dve.wait_ge(S("d_y"), g.n + 1)
                for k in range(r):
                    last = nc.vector.bn_stats(dst2[0:w, k, :], dy[0:w, k * D:(k + 1) * D])
                last.then_inc(S("d_st2"), 1)
                dve.wait_ge(S("d_st2"), g.n + 1)
                take_waits(dve)
                for k in range(r):
                    last = nc.vector.bn_aggr(dmv2[0:w, k, :], dst2[0:w, k, :])
                last.then_inc(S("d_var2"), 1)
            if stg == "norm3":
                dve.wait_ge(S("d_sd2"), g.n + 1)
                nc.vector.reciprocal(drs2[0:w, 0:r], dsd2[0:w, 0:r]).then_inc(S("d_rs2"), 1)
                dve.wait_ge(S("d_rs2"), g.n + 1)
                nc.vector.scalar_tensor_tensor(dshift[0:w, 0:r], dmv2[0:w, 0:r, 0], -1.0, drs2[0:w, 0:r],
                                               ALU.mult, ALU.mult).then_inc(S("d_shift"), 1)

        def dense_sp(sp, g, stg, free):
            if stg == "load":
                wait(sp, S("d_o_out"), free)
                sp.dma_start(xin[0:g.p, g.slot, 0:g.r * D], g.dram(x)).then_inc(d_in[g.slot], 16)
            if stg == "store":
                sp.wait_ge(S("d_z"), g.n + 1)
                sp.dma_start(g.dram(out), zout[0:g.p, g.slot, 0:g.r * D]).then_inc(d_out[g.slot], 16)

        EDGE = {"T": 0, "M": 1, "N": 2, "H": 3, "O": 4, "R": 5, "Q": 6, "W": 7}

        def edge_pe(pe, i, k, stg):
            n, b, c = step(i, k), k % 2, k % RING
            if stg == "T":
                pe.wait_ge(gat[k], gathered("edge", i))
                wait(pe, S("e_x_out"), n)
                nc.tensor.transpose(pX[:, 0:P], gx[:, k, 0, :], ident[:, :])
                nc.tensor.transpose(pX[:, P:2 * P], gx[:, k, 1, :], ident[:, :]).then_inc(S("e_x"), 1)
            if stg == "M":
                pe.wait_ge(S("e_x_out"), n + 1)
                wait(pe, S("e_m_out"), n)
                nc.tensor.matmul(pM[:, 0:D], ones96[:, :], bsplit[:, 0, :], start=True, stop=False)
                nc.tensor.matmul(pM[:, 0:D], xT[:, c, 0:P], Wa[:, :], start=False, stop=False)
                nc.tensor.matmul(pM[:, 0:D], xT[:, c, P:2 * P], Wb[:, :], start=False, stop=True
                                 ).then_inc(S("e_m"), 1)
            if stg == "N":
                pe.wait_ge(S("e_m_out"), n + 1)
                wait(pe, S("e_n_out"), n)
                nc.tensor.matmul(pS[:, 0:P], msg[:, b, :], same[:, ds(n * P, P)], start=True, stop=True
                                 ).then_inc(S("e_n"), 1)
            if stg == "H":
                pe.wait_ge(S("e_r"), n + 1)
                wait(pe, S("e_h_out"), n)
                nc.tensor.matmul(pH[:, 0:2 * P], W1s[:, :], rT[:, c, :], start=True, stop=True).then_inc(S("e_h"), 1)
            if stg == "O":
                pe.wait_ge(S("e_h_out"), n + 1)
                wait_tile(pe, "e_o_out", i, k - 1)
                nc.tensor.matmul(pO[:, 0:2 * D], ones96[:, :], bsplit[:, 1:3, :].rearrange("p a d -> p (a d)"),
                                 start=True, stop=False)
                for a in range(2):
                    last = nc.tensor.matmul(pO[:, a * D:(a + 1) * D], hT[:, b, a * P:(a + 1) * P], W2s[:, :],
                                            start=False, stop=(a == 1))
                last.then_inc(S("e_o"), 1)

        def edge_act(act, i, k, stg):
            n, b, c = step(i, k), k % 2, k % RING
            if stg == "T":
                act.wait_ge(S("e_x"), n + 1)
                wait(act, S("e_h"), n - (RING - 1))
                nc.scalar.copy(xT[:, c, :], pX[:, 0:2 * P])
                nc.scalar.activation(rT[:, c, 0:P], pX[:, 0:P], ACT.Identity, scale=eps1[:, 0:1]
                                     ).then_inc(S("e_x_out"), 1)
            if stg == "M":
                act.wait_ge(S("e_m"), n + 1)
                wait(act, S("e_n"), n - 1)
                nc.scalar.activation(msg[:, b, :], pM[:, 0:D], ACT.Relu).then_inc(S("e_m_out"), 1)
            if stg == "H":
                act.wait_ge(S("e_h"), n + 1)
                wait(act, S("e_o"), n - 1)
                nc.scalar.activation(hT[:, b, :], pH[:, 0:2 * P], ACT.Relu, bias=b1c[:, 0:1]).then_inc(S("e_h_out"), 1)
            if stg == "R":
                act.wait_ge(S("e_var"), n + 1)
                nc.scalar.activation(sd[:, b, :], mv[:, b, :, 1], ACT.Sqrt, bias=epsc[:, 0:1]).then_inc(S("e_sd"), 1)
            if stg == "Q":
                slot = k % STORES
                act.wait_ge(S("e_shift"), n + 1)
                wait(act, stored[slot], stored_before("edge", i, k))
                for a in range(2):
                    last = nc.scalar.activation(yo[:, slot, a, :], res[:, b, a, :], ACT.Identity,
                                                scale=rs[:, b, a:a + 1], bias=shift[:, b, a:a + 1])
                last.then_inc(S("e_y"), 1)

        def edge_dve(dve, i, k, stg):
            n, b, c = step(i, k), k % 2, k % RING
            if stg == "N":
                dve.wait_ge(S("e_n"), n + 1)
                nc.vector.scalar_tensor_tensor(aggT[:, b, :], cont[:, ds(n * P, P)], aggT[:, 1 - b, P - 1:P],
                                               pS[:, 0:P], ALU.mult, ALU.add).then_inc(S("e_n_out"), 1)
                dve.wait_ge(S("e_n_out"), n + 1)
                nc.vector.scalar_tensor_tensor(rT[:, c, P:2 * P], xT[:, c, P:2 * P], eps1[:, 0:1], aggT[:, b, :],
                                               ALU.mult, ALU.add).then_inc(S("e_r"), 1)
                if k % HALF == HALF - 1:
                    nc.vector.tensor_copy(deg_out[:, ds(i * BODY + k - (HALF - 1), HALF)], deg_in_flight[:, k - HALF + 1:k + 1])
            if stg == "R":
                dve.wait_ge(S("e_o"), n + 1)
                wait(dve, S("e_y"), n - 1)
                nc.vector.tensor_tensor(res[:, b, :, :].rearrange("p a d -> p (a d)"), pO[:, 0:2 * D],
                                        gx[:, k, :, :].rearrange("p a d -> p (a d)"), ALU.add
                                        ).then_inc(half_sem("e_o_out", k), 1)
                wait_tile(dve, "e_o_out", i, k)
                for a in range(2):
                    last = nc.vector.bn_stats(st[:, b, a, :], res[:, b, a, :])
                last.then_inc(S("e_st"), 1)
                dve.wait_ge(S("e_st"), n + 1)
                take_waits(dve)
                for a in range(2):
                    last = nc.vector.bn_aggr(mv[:, b, a, :], st[:, b, a, :])
                last.then_inc(S("e_var"), 1)
            if stg == "Q":
                dve.wait_ge(S("e_sd"), n + 1)
                nc.vector.reciprocal(rs[:, b, :], sd[:, b, :]).then_inc(S("e_rs"), 1)
                dve.wait_ge(S("e_rs"), n + 1)
                nc.vector.scalar_tensor_tensor(shift[:, b, :], mv[:, b, :, 0], -1.0, rs[:, b, :], ALU.mult, ALU.mult
                                               ).then_inc(S("e_shift"), 1)

        def edge_sp(sp, i, k, stg):
            n = step(i, k)
            if stg == "W":
                sp.wait_ge(S("e_y"), n + 1)
                sp.dma_start(y_dram[ds(n * (2 * P), 2 * P), :].rearrange("(p a) d -> p (a d)", a=2),
                             yo[:, k % STORES, :, :].rearrange("p a d -> p (a d)")
                             ).then_inc(stored[k % STORES], 16)

        CONV = {"S": 0, "A": 1, "B": 2, "U": 3, "Q": 4, "W": 4}

        def conv_pe(pe, c, i, k, stg):
            q, n, b = f"conv{c}", step(i, k), k % 2
            m = n + (c - 1) * T
            if stg == "A":
                pe.wait_ge(gat[k], gathered(q, i))
                if c == 1:
                    pe.wait_ge(S("c1_scaled"), n + 1)
                wait(pe, S("c_a_out"), m)
                nc.tensor.matmul(pX[:, 0:P], gx[:, k, 0, :], same[:, ds(n * P, P)], start=True, stop=True
                                 ).then_inc(half_sem("c_a", k), 1)
            if stg == "B":
                pe.wait_ge(S("c_a_out"), m + 1)
                wait(pe, S("c_b_out"), m)
                nc.tensor.matmul(pM[:, 0:D], aggT[:, b, :], Cs[c - 1][:, :], start=True, stop=True
                                 ).then_inc(S("c_b"), 1)

        def conv_dve(dve, c, i, k, stg):
            n, b = step(i, k), k % 2
            m = n + (c - 1) * T
            if stg == "A":
                wait_tile(dve, "c_a", i + (c - 1) * TURNS, k)
                wait(dve, S("c_b"), m - 1)
                wait(dve, S("c_a_out"), m)
                nc.vector.scalar_tensor_tensor(aggT[:, b, :], cont[:, ds(n * P, P)], aggT[:, 1 - b, P - 1:P],
                                               pX[:, 0:P], ALU.mult, ALU.add).then_inc(S("c_a_out"), 1)
            if stg == "B":
                dve.wait_ge(S("c_b"), m + 1)
                if c < 3:
                    wait(dve, S("c_u"), m - 1)
                nc.vector.scalar_tensor_tensor(pre[:, b, :], pM[:, 0:D], deg[:, ds(n, 1)], cb[:, c - 1, :],
                                               ALU.mult, ALU.add).then_inc(S("c_b_out"), 1)
            if stg == "U" and c == 3:
                dve.wait_ge(yd_in[k // HALF], i * (16 * HALF) + 16 * HALF)
                wait(dve, S("c3_z"), n - 1)
                dve.wait_ge(S("c_b_out"), m + 1)
                nc.vector.scalar_tensor_tensor(res[:, b, 0, :], pre[:, b, :], 0.0, yd[:, k, :], ALU.max, ALU.add
                                               ).then_inc(half_sem("c3_r", k), 1)
                wait_tile(dve, "c3_r", i, k)
                nc.vector.bn_stats(st[:, b, 0, :], res[:, b, 0, :]).then_inc(S("c3_st"), 1)
                dve.wait_ge(S("c3_st"), n + 1)
                take_waits(dve)
                nc.vector.bn_aggr(mv[:, b, 0, :], st[:, b, 0, :]).then_inc(S("c3_var"), 1)
            if stg == "Q" and c == 3:
                dve.wait_ge(S("c3_sd"), n + 1)
                nc.vector.reciprocal(rs[:, b, 0:1], sd[:, b, 0:1]).then_inc(S("c3_rs"), 1)
                dve.wait_ge(S("c3_rs"), n + 1)
                nc.vector.scalar_tensor_tensor(shift[:, b, 0:1], mv[:, b, 0, 0:1], -1.0, rs[:, b, 0:1],
                                               ALU.mult, ALU.mult).then_inc(S("c3_shift"), 1)

        def conv_act(act, c, i, k, stg):
            n, b = step(i, k), k % 2
            m = n + (c - 1) * T
            if stg == "S" and c == 1:
                nc.scalar.activation(same[:, ds(n * P, P)], same[:, ds(n * P, P)], ACT.Identity,
                                     scale=deg_out[:, ds(n, 1)]).then_inc(S("c1_scaled"), 1)
            if stg == "U" and c < 3:
                slot = k % STORES
                act.wait_ge(S("c_b_out"), m + 1)
                act.wait_ge(stored[slot], stored_before(f"conv{c}", i, k))
                nc.scalar.activation(uo[:, slot, :], pre[:, b, :], ACT.Relu).then_inc(S("c_u"), 1)
            if stg == "U" and c == 3:
                act.wait_ge(S("c3_var"), n + 1)
                nc.scalar.activation(sd[:, b, 0:1], mv[:, b, 0, 1:2], ACT.Sqrt, bias=epsc[:, 0:1]
                                     ).then_inc(S("c3_sd"), 1)
            if stg == "Q" and c == 3:
                act.wait_ge(S("c3_shift"), n + 1)
                nc.scalar.activation(gz[:, k, :], res[:, b, 0, :], ACT.Identity, scale=rs[:, b, 0:1],
                                     bias=shift[:, b, 0:1]).then_inc(S("c3_z"), 1)

        def conv_sp(sp, c, i, k, stg):
            n = step(i, k)
            m = n + (c - 1) * T
            if stg == "W" and c < 3:
                sp.wait_ge(S("c_u"), m + 1)
                sp.dma_start(u_dram[c - 1][ds(n * P, P), :], uo[:, k % STORES, :]
                             ).then_inc(stored[k % STORES], 16)

        def run(eng, count, turn):
            turn(0)
            with eng.Fori(1, count) as i:
                turn(i)

        def phase_loop(eng, phase, tile_fn, dense_fn):
            stages = EDGE if phase == "edge" else CONV
            groups = SPREAD.get(phase, 0)
            late_first = sorted(stages.items(), key=lambda kv: -kv[1])

            def steps(i, has_tiles, has_before):
                for t in range(BODY):
                    for stg, off in late_first:
                        if t >= off and has_tiles:
                            tile_fn(i, t - off, stg)
                        if t < off and has_before:
                            tile_fn(i - 1, t - off + BODY, stg)
                    for j in reversed(range(groups)):
                        for stg, off in sorted(DENSE.items(), key=lambda kv: -kv[1]):
                            due = j * BODY // groups + off
                            if due == t and has_tiles:
                                dense_fn(looped_group(phase, i, j), stg, i, j)
                            if due == t + BODY and has_before:
                                dense_fn(looped_group(phase, i - 1, j), stg, i - 1, j)

            steps(0, True, False)
            with eng.Fori(1, TURNS) as i:
                steps(i, True, True)
            steps(TURNS, False, True)

        def ahead(dense_fn):
            for t in range(2 * AHEAD + max(DENSE.values()) + 1):
                for m in range(AHEAD + 1):
                    for stg, off in DENSE.items():
                        if 2 * m + off == t:
                            dense_fn(ahead_group(m), stg)

        def free_after(phase, i, j):
            n = looped_group(phase, i, j).n
            if not isinstance(i, int):
                return n - (SPREAD[phase] - 1)
            if i > 0:
                return n - (SPREAD[phase] - 1)
            return n - j

        block = ctx.enter_context(nc.Block())

        @block.sync
        def _(sp):
            sp.wait_ge(s_pad, 1)
            for a, v in ((0, src), (1, dst)):
                sp.dma_start(rows_i[0:FULL, a, :], v[0:FULL * P].rearrange("(t p) -> t p", p=P)).then_inc(s_rows, 16)
                sp.dma_start(rows_i[FULL:FULL + 1, a, 0:E - FULL * P],
                             v[FULL * P:E].rearrange("(t p) -> t p", t=1)).then_inc(s_rows, 16)
            for tile_, w in ((Wa, W_edge[0:D, :]), (Wb, W_edge[D:2 * D, :]), (W1s, W1), (W2s, W2),
                             (Cs[0], C1), (Cs[1], C2), (Cs[2], C3)):
                sp.dma_start(tile_[:, :], w).then_inc(s_w, 16)
            sp.dma_start(b1c[:, :], b1.rearrange("(p a) -> p a", a=1)).then_inc(s_w, 16)
            sp.dma_start(eps1[:, :], eps.rearrange("(p a) -> p a", a=1).to_broadcast([P, 1])).then_inc(s_w, 16)
            for a, v in enumerate((c1, c2, c3)):
                sp.dma_start(cb[:, a, :], v.rearrange("(a d) -> a d", a=1).to_broadcast([P, D])).then_inc(s_w, 16)
            for a, v in enumerate((b_edge, b2)):
                sp.dma_start(braw[:, a, :], v.rearrange("(a d) -> a d", a=1).to_broadcast([96, D])).then_inc(s_w, 16)
            sp.wait_ge(s_padded, 1)
            for a in range(2):
                sp.dma_start(ids_dram[a, 1:1 + EP].rearrange("(t p) -> t p", p=P), rows[:, a, :]).then_inc(s_ids, 16)
            sp.dma_start(ids_dram[1:2, 0:1], part[0:1, 0:1]).then_inc(s_ids, 16)
            sp.dma_start(ids_dram[1:2, EP + 1:EP + 2], tab[0:1, 0:1]).then_inc(s_ids, 16)
            sp.wait_ge(s_ids, 16 * 4)
            sp.dma_start(rows[:, 3, :], ids_dram[1, 2:2 + EP].rearrange("(t p) -> t p", p=P)).then_inc(s_srt, 16)
            sp.dma_start(srt[:, 0, 0:1], ids_dram[1, 0:EP].rearrange("(t p) -> t p", p=P)[:, 0:1]).then_inc(s_srt, 16)
            sp.dma_start(srt[:, 0, 1:1 + P], ids_dram[1, 1:1 + EP].rearrange("(t p) -> t p", p=P)).then_inc(s_srt, 16)
            sp.dma_start(srt[1:T, 1, 0:1], ids_dram[1, 0:EP - P].rearrange("(t p) -> t p", p=P)[:, 0:1]).then_inc(s_srt, 16)
            sp.dma_start(srt[1:T, 1, 1:1 + P], ids_dram[1, 1:1 + EP - P].rearrange("(t p) -> t p", p=P)).then_inc(s_srt, 16)
            sp.wait_ge(s_ci, 1)
            for a in range(2):
                sp.dma_start(u_dram[a][EP:EP + 1, :], relu_cb[0:1, a, :]).then_inc(s_const_u, 16)
            sp.wait_ge(S("v_tab"), 1)
            for a in range(2):
                sp.dma_start(count_dram[a * T * LO:(a + 1) * T * LO, :].rearrange("(p l) o -> p (l o)", l=LO),
                             tab[:, a * LO:(a + 1) * LO]).then_inc(s_table, 16)

            def spread_ids(i):
                wait(sp, s_bcused, i)
                for a, ids_bc, w in ((0, src_bc, T), (1, dst_bc, P)):
                    sp.dma_start(ids_bc[:, :], ids_dram[a:a + 1, ds(i * CH + 1, CH)].to_broadcast([w, CH])
                                 ).then_inc(s_bc, 16)
            run(sp, TURNS, spread_ids)
            sp.wait_ge(s_bcused, TURNS)
            ahead(lambda g, stg: dense_sp(sp, g, stg, g.n - SLOTS + 1))
            phase_loop(sp, "edge", lambda i, k, stg: edge_sp(sp, i, k, stg),
                       lambda g, stg, i, j: dense_sp(sp, g, stg, free_after("edge", i, j)))
            for c in (1, 2):
                phase_loop(sp, f"conv{c}", lambda i, k, stg: conv_sp(sp, c, i, k, stg),
                           lambda g, stg, i, j: dense_sp(sp, g, stg, free_after(f"conv{c}", i, j)))

            def load_y(i):
                for k in range(BODY):
                    n = step(i, k)
                    if k % HALF == 0:
                        wait(sp, half_sem("c3_r", k), i * HALF)
                    sp.dma_start(yd[:, k, :], y_dram[ds(n * (2 * P), 2 * P), :].rearrange(
                        "(p a) d -> p a d", a=2)[:, 1, :]).then_inc(yd_in[k // HALF], 16)
            run(sp, TURNS, load_y)
            for k in range(BODY):
                sp.wait_ge(gat[k], gathered("conv3", TURNS - 1) + 16)

        @block.gpsimd
        def _(pool):
            nc.gpsimd.memset(rows_i[:, 0, :], SRC_PAD)
            nc.gpsimd.memset(rows_i[:, 1, :], DST_PAD).then_inc(S("g_m"), 1)
            nc.gpsimd.memset(ident[:, :], 0.0)
            nc.gpsimd.memset(last_row[:, :], 1.0).then_inc(S("g_z"), 1)
            nc.gpsimd.iota(enum_i[:, :], [[P, T]], base=0, channel_multiplier=1)
            nc.gpsimd.iota(ramp_i[:, :], [[1, LO]], base=0, channel_multiplier=0)
            nc.gpsimd.iota(part_i[:, :], [[0, 1]], base=0, channel_multiplier=1).then_inc(s_iota, 1)
            pool.wait_ge(S("g_z"), 1)
            pool.wait_ge(S("g_m"), 1)
            nc.gpsimd.affine_select(out=ident[:, :], in_=ident[:, :], compare_op=ALU.not_equal, fill=1.0, base=0,
                                    pattern=[[-1, P]], channel_multiplier=1).then_inc(s_pad, 1)
            nc.gpsimd.affine_select(out=last_row[:, :], in_=last_row[:, :], compare_op=ALU.is_ge, fill=0.0,
                                    base=-(P - 1), pattern=[[0, P]], channel_multiplier=1).then_inc(s_iota, 1)
            pool.wait_ge(S("v_runs"), 1)
            nc.gpsimd.affine_select(out=runs[:, :], in_=runs[:, :], compare_op=ALU.is_ge, fill=0.0, base=0,
                                    pattern=[[1, T]], channel_multiplier=-1).then_inc(S("g_runs"), 1)

            def halves(h):
                return range(h * HALF, (h + 1) * HALF)

            def take_indices(to, column, i, h, signal, count):
                take_waits(pool)
                nc.gpsimd.tensor_copy(to[:, h * HALF:(h + 1) * HALF], idx[:, column, ds(i * BODY + h * HALF, HALF)]
                                      ).then_inc(signal, 1)
                pool.wait_ge(signal, count)
                take_waits(pool)

            def gather(to, table, index):
                return nc.gpsimd.indirect_dma_start(to, None, table, bass.IndirectOffsetOnAxis(ap=index, axis=0))

            def edge_gathers(i):
                for h in range(2):
                    wait(pool, S(f"e_o_out_{h}"), i * HALF)
                    take_indices(stage[:, 1, :], DST_I, i, h, S("g_dst"), i * 2 + h + 1)
                    take_indices(stage[:, 0, :], SRC_I, i, h, S("g_src"), i * 2 + h + 1)
                    for k in halves(h):
                        gather(gx[:, k, 0, :], x, stage[:, 0, k:k + 1]).then_inc(gat[k], 16)
                        gather(gx[:, k, 1, :], x, stage[:, 1, k:k + 1]).then_inc(gat[k], 16)
                        gather(deg_in_flight[:, k:k + 1], count_dram, stage[:, 0, k:k + 1]).then_inc(gat[k], 16)

            def conv_gathers(c, i, h):
                wait(pool, S(f"c_a_{h}"), i * HALF + (c - 1) * (TURNS * HALF))
                take_indices(stage[:, 0, :], Y_I if c == 1 else U_I, i, h, S("g_row"), (i + (c - 1) * TURNS) * 2 + h + 1)
                for k in halves(h):
                    gather(gx[:, k, 0, :], (y_dram, u_dram[0], u_dram[1])[c - 1], stage[:, 0, k:k + 1]
                           ).then_inc(gat[k], 16)

            def scatters(i, h):
                for k in halves(h):
                    pool.wait_ge(gat[k], gathered("conv3", i))
                take_indices(ostage, O_I, i, h, S("g_out"), i * 2 + h + 1)
                for k in halves(h):
                    pool.wait_ge(S("c3_z"), i * BODY + (k + 1))
                    take_waits(pool)
                    nc.gpsimd.indirect_dma_start(
                        out, bass.IndirectOffsetOnAxis(ap=ostage[:, k:k + 1], axis=0), gz[:, k, :], None,
                        bounds_check=N - 1, oob_is_err=False).then_inc(gat[k], 16)

            pool.wait_ge(S("v_idx"), 1)
            pool.wait_ge(s_table, 32)
            run(pool, TURNS, edge_gathers)
            all_stored(pool, "edge")
            pool.wait_ge(S("v_rowidx"), 1)
            run(pool, TURNS, lambda i: (conv_gathers(1, i, 0), conv_gathers(1, i, 1)))
            all_stored(pool, "conv1")
            pool.wait_ge(s_const_u, 32)
            run(pool, TURNS, lambda i: (conv_gathers(2, i, 0), conv_gathers(2, i, 1)))
            all_stored(pool, "conv2")
            for j in range(SLOTS):
                pool.wait_ge(d_out[j], 16 * (len(range(j, AHEAD + 1, SLOTS)) + turns_of_slot(PHASES[:3], j)))

            conv_gathers(3, 0, 0)
            conv_gathers(3, 0, 1)
            scatters(0, 0)
            with pool.Fori(1, TURNS) as i:
                conv_gathers(3, i, 0)
                scatters(i - 1, 1)
                conv_gathers(3, i, 1)
                scatters(i, 0)
            scatters(TURNS - 1, 1)

        @block.vector
        def _(dve):
            count = [0]

            def link(ins):
                count[0] += 1
                ins.then_inc(s_v, 1)
                dve.wait_ge(s_v, count[0])

            V = nc.vector
            V.memset(zeros[:, :], 0.0)
            V.memset(ones96[:, :], 0.0)
            V.memset(bsplit[:, :, :], 0.0)
            V.memset(epsc[:, :], EPS)
            V.memset(aggT[:, :, :], 0.0)
            V.memset(srt[:, :, :], 0.0)
            link(V.memset(tab[0:1, 0:1], float(DST_END)))
            for q in range(3):
                V.memset(ones96[32 * q:32 * q + 1, :], 1.0)
            dve.wait_ge(s_iota, 2)
            V.tensor_copy(enum[:, :], enum_i[:, :])
            V.tensor_copy(ramp[:, :], ramp_i[:, :])
            link(V.memset(part[:, 0:1], -1.0))
            link(V.tensor_copy(part[:, 1:2], part_i[:, :]))
            dve.wait_ge(s_rows, 64)
            V.tensor_copy(rows[:, 0, :], rows_i[:, 0, :])
            V.tensor_copy(rows[:, 1, :], rows_i[:, 1, :])
            link(V.tensor_scalar(tmp_i[:, :], rows_i[:, 0, :], 8, None, ALU.logical_shift_right))
            V.tensor_copy(rows[:, 2, :], tmp_i[:, :]).then_inc(s_padded, 1)
            dve.wait_ge(s_padded, 1)
            dve.wait_ge(s_pe, 1)
            link(V.tensor_copy(cols[:, 0:3, :], pX[:, 0:3 * T].rearrange("p (a t) -> p a t", a=3)))
            V.scalar_tensor_tensor(cols[:, 3, :], cols[:, 2, :], -float(LO), cols[:, 0, :], ALU.mult, ALU.add)
            V.tensor_scalar(idx[:, SRC_I, :], cols[:, 0, :], float(N - 1), None, ALU.min)
            link(V.tensor_scalar(idx[:, DST_I, :], cols[:, 1, :], float(N - 1), None, ALU.min))
            V.memset(first_bc[:, 0:1], -1.0).then_inc(S("v_idx"), 1)
            dve.wait_ge(s_pe, 2)
            link(V.tensor_copy(first_bc[:, 1:T], pM[:, 0:T - 1]))
            V.tensor_scalar(runs[:, :], pM[0:T, 0:T], rows[:, 1, P - 1:P], None, ALU.is_equal).then_inc(S("v_runs"), 1)
            dve.wait_ge(s_srt, 80)
            dve.wait_ge(s_pe, 3)
            link(V.tensor_copy(cols[:, 4, :], pX[:, 3 * T:4 * T]))
            link(V.tensor_tensor(fidx[:, 0, :], cols[:, 1, :], cols[:, 4, :], ALU.is_equal))
            link(V.scalar_tensor_tensor(idx[:, O_I, :], fidx[:, 0, :], 65536.0, cols[:, 1, :], ALU.mult, ALU.add))
            V.tensor_copy(before[:, :], srt[:, 0, 0:1])
            link(V.tensor_scalar(srt[:, 0, P + 1:P + 2], part[0:T, 1:2], float(P), None, ALU.mult))
            link(V.tensor_scalar(srt[:, 1, P + 1:P + 2], srt[:, 0, P + 1:P + 2], -float(P), 0.0, ALU.add, ALU.max))
            link(V.tensor_tensor(srt[:, 0, :], srt[:, 0, :], srt[:, 1, :], ALU.subtract))
            link(V.tensor_copy(srt_i[:, :], srt[:, 0, :]))
            link(V.tensor_scalar(srt_i[:, :], srt_i[:, :], 255, None, ALU.bitwise_and))
            link(V.tensor_copy(step_lo[:, :], srt_i[:, :]))
            link(V.tensor_tensor(step_hi[:, :], srt[:, 0, :], step_lo[:, :], ALU.subtract))
            dve.wait_ge(s_w, 16 * 14)
            link(V.tensor_scalar(eps1[:, :], eps1[:, :], 1.0, None, ALU.add))
            V.tensor_scalar(relu_cb[:, :, :], cb[:, :, :], 0.0, None, ALU.max).then_inc(s_ci, 1)
            link(V.tensor_copy(bhalf[:, :, :], braw[:, :, :]))
            for q in range(3):
                r_ = slice(32 * q, 32 * q + 1)
                V.tensor_copy(bsplit[r_, 0, :], bhalf[r_, 0, :])
                link(V.tensor_copy(bsplit[r_, 1:5, :], bhalf[r_, 1, :].unsqueeze(1).to_broadcast([1, 4, D])))
                if q < 2:
                    link(V.tensor_tensor(braw[:, :, :], braw[:, :, :], bhalf[:, :, :], ALU.subtract))
                    link(V.tensor_copy(bhalf[:, :, :], braw[:, :, :]))
            V.memset(bres[:, :, :], 0.0).then_inc(S("v_bias"), 1)
            def one_hot(i):
                for b in range(2):
                    wait(dve, s_hist, i * 2 + b - 1)
                    V.tensor_scalar(hot_hi[:, b, :], ramp[:, 0:HI], cols[:, 2, ds(i * 2 + b, 1)], None, ALU.is_equal)
                    V.tensor_scalar(hot_lo[:, b, :], ramp[:, :], cols[:, 3, ds(i * 2 + b, 1)], None, ALU.is_equal
                                    ).then_inc(s_hot, 1)
            run(dve, T // 2, one_hot)
            dve.wait_ge(s_pe, 4)
            V.tensor_copy(tab[:, :], pH[0:T, :]).then_inc(S("v_tab"), 1)

            def chunk(i):
                dve.wait_ge(s_bc, i * 32 + 32)
                wait(dve, s_look, i * BODY)
                V.tensor_scalar(above[:, :], src_bc[:, :], before[:, 0:1], None, ALU.is_ge).then_inc(s_hi, 1)
                view = dst_bc[:, :].rearrange("p (t f) -> p t f", f=P)
                V.tensor_tensor(same[:, ds(i * CH, CH)].rearrange("p (t f) -> p t f", f=P), view,
                                cols[:, 1, ds(i * BODY, BODY)].unsqueeze(2).to_broadcast([P, BODY, P]), ALU.is_equal
                                ).then_inc(S("v_same"), 1)
                V.tensor_tensor(cont[:, ds(i * CH, CH)].rearrange("p (t f) -> p t f", f=P), view,
                                first_bc[:, ds(i * BODY, BODY)].unsqueeze(2).to_broadcast([P, BODY, P]), ALU.is_equal
                                ).then_inc(s_bcused, 1)
                dve.wait_ge(S("v_same"), i + 1)
                V.tensor_reduce(own[:, ds(i * BODY, BODY)], same[:, ds(i * CH, CH)].rearrange("p (t f) -> p t f", f=P),
                                AX.X, ALU.add).then_inc(S("v_own"), 1)
                for k in range(BODY):
                    n, b = step(i, k), k % 2
                    pc = (pO, pM)[b]
                    dve.wait_ge(s_look, n + 1)
                    wait(dve, s_looked, n - 1)
                    V.tensor_scalar(junk2[:, b, 0, 0:P], pc[:, 1:1 + P], cols[:, 0, ds(n, 1)], pc[:, P + 1:P + 2],
                                    ALU.is_le, ALU.add, accum_out=below[:, ds(n, 1)])
                    V.tensor_scalar(junk2[:, b, 1, :], pc[:, 0:1 + P], cols[:, 0, ds(n, 1)], None, ALU.is_equal,
                                    ALU.add, accum_out=equal[:, ds(n, 1)]).then_inc(s_looked, 1)
            run(dve, TURNS, chunk)
            dve.wait_ge(s_looked, T)
            dve.wait_ge(s_pe, 5)
            V.tensor_copy(ends[:, :], pS[0:T, 0:P]).then_inc(S("v_ends"), 1)
            dve.wait_ge(s_pe, 6)
            link(V.tensor_tensor(deg[:, :], cols[:, 1, :], first_bc[:, :], ALU.is_equal))
            link(V.tensor_tensor(deg[:, 1:T], deg[:, 1:T], pS[:, P:P + T - 1], ALU.mult))
            link(V.tensor_tensor(deg[:, :], deg[:, :], own[:, :], ALU.add))
            V.tensor_scalar(deg[:, :], deg[:, :], 1.0, None, ALU.max).then_inc(S("v_deg"), 1)
            dve.wait_ge(s_root, 1)
            V.reciprocal(deg[:, :], deg[:, :])
            link(V.tensor_scalar(hit[:, :], equal[:, :], 1.0, None, ALU.min))
            link(V.tensor_scalar(fidx[:, 1, :], below[:, :], -float(EP + 1), None, ALU.add))
            link(V.tensor_tensor(fidx[:, 1, :], fidx[:, 1, :], hit[:, :], ALU.mult))
            link(V.tensor_scalar(idx[:, U_I, :], fidx[:, 1, :], float(EP), None, ALU.add))
            link(V.tensor_tensor(fidx[:, 0, :], below[:, :], enum[:, :], ALU.subtract))
            link(V.tensor_scalar(fidx[:, 0, :], fidx[:, 0, :], 2.0, -1.0, ALU.mult, ALU.add))
            link(V.tensor_tensor(fidx[:, 0, :], fidx[:, 0, :], hit[:, :], ALU.mult))
            link(V.scalar_tensor_tensor(idx[:, Y_I, :], enum[:, :], 2.0, fidx[:, 0, :], ALU.mult, ALU.add))
            V.memset(bres[:, 0, 0:1], 0.0).then_inc(S("v_rowidx"), 1)

            ahead(lambda g, stg: dense_dve(dve, g, stg))
            phase_loop(dve, "edge", lambda i, k, stg: edge_dve(dve, i, k, stg),
                       lambda g, stg, i, j: dense_dve(dve, g, stg))
            dve.wait_ge(S("e_y"), T)
            V.tensor_scalar(deg_out[:, :], deg_out[:, :], 1.0, None, ALU.max).then_inc(S("v_deg"), 1)
            dve.wait_ge(s_root, 2)
            V.reciprocal(deg_out[:, :], deg_out[:, :]).then_inc(S("v_scale"), 1)
            for c in (1, 2, 3):
                phase_loop(dve, f"conv{c}", lambda i, k, stg: conv_dve(dve, c, i, k, stg),
                           lambda g, stg, i, j: dense_dve(dve, g, stg))

        @block.scalar
        def _(act):
            act.wait_ge(S("v_deg"), 1)
            nc.scalar.activation(deg[:, :], deg[:, :], ACT.Sqrt).then_inc(s_root, 1)
            ahead(lambda g, stg: dense_act(act, g, stg))
            phase_loop(act, "edge", lambda i, k, stg: edge_act(act, i, k, stg),
                       lambda g, stg, i, j: dense_act(act, g, stg))
            act.wait_ge(S("v_deg"), 2)
            nc.scalar.activation(deg_out[:, :], deg_out[:, :], ACT.Sqrt).then_inc(s_root, 1)
            act.wait_ge(S("v_scale"), 1)
            for c in (1, 2, 3):
                phase_loop(act, f"conv{c}", lambda i, k, stg: conv_act(act, c, i, k, stg),
                           lambda g, stg, i, j: dense_act(act, g, stg))

        @block.tensor
        def _(pe):
            pe.wait_ge(s_iota, 2)
            pe.wait_ge(s_padded, 1)
            for a in range(3):
                last = nc.tensor.transpose(pX[:, a * T:(a + 1) * T], rows[:, a, :], ident[0:T, 0:T])
            last.then_inc(s_pe, 1)
            pe.wait_ge(S("v_idx"), 1)
            nc.tensor.matmul(pM[:, 0:T], last_row[:, :], cols[:, 1, :], start=True, stop=True).then_inc(s_pe, 1)
            pe.wait_ge(s_srt, 80)
            nc.tensor.transpose(pX[:, 3 * T:4 * T], rows[:, 3, :], ident[0:T, 0:T]).then_inc(s_pe, 1)
            pe.wait_ge(S("v_bias"), 1)
            nc.tensor.matmul(pH[0:T, :], zeros[:, 0:T], zeros[:, :], start=True, stop=False)

            def count(i):
                for b in range(2):
                    pe.wait_ge(s_hot, i * 2 + b + 1)
                    for a in range(2):
                        last = nc.tensor.matmul(pH[0:T, a * LO:(a + 1) * LO], hot_hi[:, b, a * T:(a + 1) * T],
                                                hot_lo[:, b, :], start=False, stop=False)
                    last.then_inc(s_hist, 1)
            run(pe, T // 2, count)
            nc.tensor.matmul(pH[0:T, :], zeros[:, 0:T], zeros[:, :], start=False, stop=True).then_inc(s_pe, 1)

            def look_up(i):
                pe.wait_ge(s_hi, i + 1)
                for k in range(BODY):
                    n, b = step(i, k), k % 2
                    pc, cs = (pO, pM)[b], slice(k * P, (k + 1) * P)
                    wait(pe, s_looked, n - 1)
                    nc.tensor.matmul(pc[:, 0:P + 2], above[:, cs], step_lo[:, :], start=True, stop=False)
                    nc.tensor.matmul(pc[:, 0:P + 2], above[:, cs], step_hi[:, :], start=False, stop=True
                                     ).then_inc(s_look, 1)
            run(pe, TURNS, look_up)
            pe.wait_ge(S("v_own"), TURNS)
            nc.tensor.matmul(pS[0:T, 0:P], own[:, :], last_row[:, :], start=True, stop=True).then_inc(s_pe, 1)
            pe.wait_ge(S("v_ends"), 1)
            pe.wait_ge(S("g_runs"), 1)
            nc.tensor.matmul(pS[:, P:P + T], ends[:, :], runs[:, :], start=True, stop=True).then_inc(s_pe, 1)
            pe.wait_ge(S("v_rowidx"), 1)

            ahead(lambda g, stg: dense_pe(pe, g, stg))
            phase_loop(pe, "edge", lambda i, k, stg: edge_pe(pe, i, k, stg),
                       lambda g, stg, i, j: dense_pe(pe, g, stg))
            for c in (1, 2, 3):
                phase_loop(pe, f"conv{c}", lambda i, k, stg: conv_pe(pe, c, i, k, stg),
                           lambda g, stg, i, j: dense_pe(pe, g, stg))


_INS = ["x", "src", "dst", "L0_gnn_W_edge", "L0_gnn_b_edge", "L0_gnn_W1", "L0_gnn_b1", "L0_gnn_W2", "L0_gnn_b2",
        "L0_gnn_eps", "L1_gnn_W1", "L1_gnn_b1", "L1_gnn_W2", "L1_gnn_b2", "L1_gnn_W3", "L1_gnn_b3"]


def kernel(**inputs):
    import numpy as _np
    import concourse.bacc as _bacc
    from concourse import mybir as _mybir
    from concourse.bass_utils import run_bass_kernel_spmd as _run

    nc = _bacc.Bacc("TRN2", target_bir_lowering=False, num_devices=1)
    arrays, args = {}, []
    for name in _INS:
        a = _np.ascontiguousarray(inputs[name])
        arrays[f"in_{name}"] = a
        args.append(nc.dram_tensor(f"in_{name}", a.shape, _mybir.dt.from_np(a.dtype), kind="ExternalInput").ap())
    args.append(nc.dram_tensor("out", (N, D), _mybir.dt.float32, kind="ExternalOutput").ap())
    build(nc, *args)
    r = _run(nc, [arrays], core_ids=[0])
    return r.results[0]["out"]
```

```python
import concourse.bass as bass
from concourse import mybir
from contextlib import ExitStack

N = 50000
E = 12500
D = 128
P = 128
T = -(-E // P)
EP = T * P
BODY = 14
TURNS = T // BODY
CH = BODY * P
FULL = E // P
HI, LO = 2 * T, 256
SRC_PAD = HI * LO - 1
DST_PAD, DST_END = 65535, 70000
G = 512
R = G // P
SPREAD = {"edge": 5, "conv1": 4, "conv2": 4}
LOOPED = TURNS * sum(SPREAD.values())
AHEAD = N // G - LOOPED
TAIL = N - (N // G) * G
TP = TAIL // 3
RING = 7
SLOTS = 5
STORES = 4
LOOKS = 4
LAG = 11
COUNTED = 4
EPS = 1e-5

STAGES = {"load": 0, "T": 3, "T_out": 4, "H": 5, "H_out": 6, "O": 7, "add": 8, "stats1": 9, "var1": 9,
          "sd1": 10, "rsd1": 11, "y": 11, "stats2": 12, "var2": 12, "sd2": 13, "rsd2": 14, "shift": 14,
          "norm": 15, "store": 15}
DENSE = {"edge": STAGES, "conv1": STAGES, "conv2": STAGES}
EDGE = {"T": 0, "T_out": 0, "M": 1, "M_out": 1, "N": 2, "N_out": 2, "in": 2, "H": 3, "H_out": 3, "O": 4,
        "add": 4, "stats": 5, "var": 5, "sd": 6, "rsd": 7, "shift": 7, "norm": 8, "store": 8}
CONV = {"scale": 0, "A": 1, "A_out": 2, "B": 3, "relu": 4, "store": 4}
CONV3 = {"A": 1, "A_out": 2, "B": 3, "add": 4, "stats": 5, "var": 5, "sd": 6, "rsd": 7, "shift": 7, "norm": 8}
SECOND = {"in", "var", "shift", "var1", "y", "var2"}




def build(nc, x, src, dst, W_edge, b_edge, W1, b1, W2, b2, eps, C1, c1, C2, c2, C3, c3, out):
    f32, bf16, i32 = mybir.dt.float32, mybir.dt.bfloat16, mybir.dt.int32
    ALU, ACT, AX = mybir.AluOpType, mybir.ActivationFunctionType, mybir.AxisListType
    ds = bass.ds
    ctx = ExitStack()
    with ctx:
        ctx.enter_context(nc.allow_non_contiguous_dma(reason="columns of biases and of edge ids, once"))

        def sb(name, shape, dt=f32):
            return ctx.enter_context(nc.sbuf_tensor(name, shape, dt))

        def sem(name):
            return ctx.enter_context(nc.semaphore(name))

        count_dram = nc.dram_tensor("count_dram", [HI * LO, 1], f32, kind="Internal").ap()
        ids_dram = nc.dram_tensor("ids_dram", [2, EP + 2], f32, kind="Internal").ap()
        y_dram = nc.dram_tensor("y_dram", [EP * 2, D], f32, kind="Internal").ap()
        u_dram = [nc.dram_tensor(f"u{n}_dram", [EP + 1, D], f32, kind="Internal").ap() for n in (1, 2)]

        same = sb("same", [P, EP])
        cont = sb("cont", [P, EP], bf16)
        above_a = sb("above_a", [T, CH], bf16)
        rows_i = sb("rows_i", [T, 2, P], i32)
        rows = sb("rows", [T, 4, P])
        tmp_i = sb("tmp_i", [T, P], i32)
        cols = sb("cols", [P, 5, T])
        srt = sb("srt", [T, 2, P + 2])
        srt_i = sb("srt_i", [T, P + 2], i32)
        before = sb("before", [T, 1])
        step_lo = sb("step_lo", [T, P + 2], bf16)
        step_hi = sb("step_hi", [T, P + 2], bf16)
        first_bc = sb("first_bc", [P, T])
        runs = sb("runs", [T, 2, T])
        next_bc = sb("next_bc", [P, T])
        own = sb("own", [P, T])
        ends = sb("ends", [T, 2, P])
        deg = sb("deg", [P, T])
        scale = sb("scale", [P, T])
        deg_after = sb("deg_after", [P, T])
        deg_out = sb("deg_out", [P, T])
        below = sb("below", [P, T])
        equal = sb("equal", [P, T])
        hit = sb("hit", [P, T])
        found = sb("found", [P, T])
        found_i = sb("found_i", [P, 2, T], i32)
        reach = sb("reach", [P, T])
        fidx = sb("fidx", [P, 2, T])
        idx = sb("idx", [P, 5, T], i32)
        SRC_I, DST_I, Y_I, U_I, O_I = range(5)
        stage = sb("stage", [P, 3, BODY], i32)
        ostage = sb("ostage", [P, BODY], i32)
        enum_i = sb("enum_i", [P, T], i32)
        enum = sb("enum", [P, T])
        ramp_i = sb("ramp_i", [P, LO], i32)
        ramp = sb("ramp", [P, LO], bf16)
        part_i = sb("part_i", [P, 1], i32)
        part = sb("part", [P, 3])
        ident = sb("ident", [P, P])
        last_row = sb("last_row", [P, P])
        first_row = sb("first_row", [P, P])
        hot_hi = sb("hot_hi", [P, RING, HI], bf16)
        hot_lo = sb("hot_lo", [P, RING, LO], bf16)
        tab = sb("tab", [T, 2 * LO])
        zeros = sb("zeros", [P, 512], bf16)
        mark = sb("mark", [P, 1])
        ones96 = sb("ones96", [96, P], bf16)
        braw = sb("braw", [96, 5, D])
        bhalf = sb("bhalf", [96, 5, D], bf16)
        bsplit = sb("bsplit", [96, 8, D], bf16)
        Wa, Wb, W1s, W2s = sb("Wa", [D, D]), sb("Wb", [D, D]), sb("W1s", [D, D]), sb("W2s", [D, D])
        Cs = [sb(f"C{n}s", [D, D]) for n in (1, 2, 3)]
        b1c = sb("b1c", [D, 1])
        eps1 = sb("eps1", [P, 1])
        epsc = sb("epsc", [P, 1])
        cb = sb("cb", [P, 3, D])
        relu_cb = sb("relu_cb", [P, 3, D])
        gx = sb("gx", [P, BODY, 2, D])
        gz = sb("gz", [P, BODY, D])
        yd = sb("yd", [P, BODY, D])
        deg_in_flight = sb("deg_in_flight", [P, BODY])
        xT = sb("xT", [P, RING, 2 * P])
        msg = sb("msg", [P, 2, D])
        aggT = sb("aggT", [P, 2, P])
        rT = sb("rT", [P, RING, 2 * P])
        hT = sb("hT", [P, 2, 2 * P])
        res = sb("res", [P, RING, 2, D])
        st = sb("st", [P, RING, 2, 6])
        mv = sb("mv", [P, RING, 2, 2])
        sd = sb("sd", [P, RING, 2])
        rs = sb("rs", [P, RING, 2])
        shift = sb("shift", [P, RING, 2])
        yo = sb("yo", [P, STORES, 2, D])
        uo = sb("uo", [P, STORES, D])
        xin = sb("xin", [P, SLOTS, R * D])
        zout = sb("zout", [P, SLOTS, R * D])
        dst_bc = [yd[:, :, :].rearrange("p k f -> p (k f)"), rT[:, :, :].rearrange("p k f -> p (k f)")]
        src_bc = [gz[:, :, :].rearrange("p k f -> p (k f)")[0:T, :], xT[:, :, :].rearrange("p k f -> p (k f)")[0:T, :]]
        looked = [res[:, b, :, :].rearrange("p a d -> p (a d)")[:, 0:P + 1] for b in range(LOOKS)]
        above = [above_a[:, :], hot_lo[:, :, :].rearrange("p b l -> p (b l)")[0:T, :]]
        drT = sb("drT", [P, G])
        dhT = sb("dhT", [P, G])
        dst1 = sb("dst1", [P, SLOTS, R, 6])
        dshift = sb("dshift", [P, SLOTS, R])
        dmv = sb("dmv", [P, SLOTS, R, 2])
        dsd = sb("dsd", [P, SLOTS, R])
        drs = sb("drs", [P, SLOTS, R])
        dst2 = sb("dst2", [P, SLOTS, R, 6])
        dmv2 = sb("dmv2", [P, SLOTS, R, 2])
        dsd2 = sb("dsd2", [P, SLOTS, R])
        drs2 = sb("drs2", [P, SLOTS, R])

        bank = [ctx.enter_context(nc.psum_tensor(f"bank{n}", [P, 512], f32)) for n in range(8)]
        pX, pM, pS, pH, pO, dX, dH, dO = bank
        look_banks = (pO, pM, dX, dH)

        s_w = sem("s_w")
        s_rows = sem("s_rows")
        s_iota = sem("s_iota")
        s_padded = sem("s_padded")
        s_v = sem("s_v")
        s_ids = sem("s_ids")
        s_pad = sem("s_pad")
        s_srt = sem("s_srt")
        s_pe = sem("s_pe")
        s_hot = sem("s_hot")
        s_hist = sem("s_hist")
        s_bc = [sem(f"s_bc_{a}") for a in range(2)]
        s_bcused = sem("s_bcused")
        s_hi = sem("s_hi")
        s_table = sem("s_table")
        s_look = sem("s_look")
        s_looked = sem("s_looked")
        s_root = sem("s_root")
        s_ci = sem("s_ci")
        s_const_u = sem("s_const_u")
        s_held = sem("s_held")
        PHASES = ["edge", "conv1", "conv2", "conv3"]
        HALF = BODY // 2
        gat = [sem(f"gat_{k}") for k in range(BODY)]
        stored = [sem(f"stored_{k}") for k in range(STORES)]
        yd_in = [sem(f"yd_in_{h}") for h in range(2)]
        s_counts = [sem(f"s_counts_{h}") for h in range(2)]
        d_in = [sem(f"d_in_{k}") for k in range(SLOTS)]
        d_out = [sem(f"d_out_{k}") for k in range(SLOTS)]
        ev = {}

        def S(name):
            if name not in ev:
                ev[name] = sem(name)
            return ev[name]

        def wait(eng, semaphore, value):
            if not isinstance(value, int) or value > 0:
                eng.wait_ge(semaphore, value)

        def take_waits(eng):
            eng.sem_inc(s_held, 1)

        def step(i, k):
            return i * BODY + k

        def gathered(phase, i):
            if phase == "edge":
                return i * 32 + 32
            before = TURNS * (32 + 16 * (int(phase[4]) - 1))
            return i * 32 + (before + 16) if phase == "conv3" else i * 16 + (before + 16)

        def turns(k, slots=BODY):
            return len(range(k, BODY, slots))

        def stored_before(phase, i, k):
            slot = k % STORES
            return i * (16 * turns(slot, STORES)) + 16 * (k // STORES + PHASES.index(phase) * TURNS * turns(slot, STORES))

        def all_stored(eng, phase):
            for slot in range(STORES):
                eng.wait_ge(stored[slot], 16 * turns(slot, STORES) * TURNS * (PHASES.index(phase) + 1))

        def half_sem(name, k):
            return S(f"{name}_{k // HALF}")

        def wait_tile(eng, name, i, k):
            if k < 0:
                wait(eng, half_sem(name, BODY + k), i * HALF + (k + 1))
            else:
                wait(eng, half_sem(name, k), i * HALF + (k % HALF + 1))

        class Group:
            def __init__(self, n, slot, uses, rows_, parts, start):
                self.n, self.slot, self.uses, self.r, self.p, self.start = n, slot, uses, rows_, parts, start

            def dram(self, a):
                return a[ds(self.start, self.r * self.p), :].rearrange("(p k) d -> p (k d)", k=self.r)

        def ahead_group(m):
            if m == AHEAD:
                return Group(m, m % SLOTS, m // SLOTS, 3, TP, (N // G) * G)
            return Group(m, m % SLOTS, m // SLOTS, R, P, m * G)

        def turns_of_slot(phases, j):
            return TURNS * sum(j < SPREAD[q] for q in phases)

        def looped_group(phase, i, j):
            earlier = PHASES[:PHASES.index(phase)]
            groups = TURNS * sum(SPREAD[q] for q in earlier)
            uses = len(range(j, AHEAD + 1, SLOTS)) + turns_of_slot(earlier, j)
            return Group(i * SPREAD[phase] + (groups + AHEAD + 1 + j), j, i + uses, R, P,
                         i * (SPREAD[phase] * G) + (AHEAD + groups + j) * G)

        def dense_pe(pe, g, stg):
            w, r = g.p, g.r
            if stg == "T":
                pe.wait_ge(d_in[g.slot], g.uses * 16 + 16)
                wait(pe, S("d_xT_out"), g.n)
                for k in range(r):
                    last = nc.tensor.transpose(dX[:, k * w:(k + 1) * w], xin[0:w, g.slot, k * D:(k + 1) * D],
                                               ident[0:w, 0:w])
                last.then_inc(S("d_xT"), 1)
            if stg == "H":
                pe.wait_ge(S("d_xT_out"), g.n + 1)
                wait(pe, S("d_h_out"), g.n)
                nc.tensor.matmul(dH[:, 0:r * w], W1s[:, :], drT[:, 0:r * w], start=True, stop=True
                                 ).then_inc(S("d_h"), 1)
            if stg == "O":
                pe.wait_ge(S("d_h_out"), g.n + 1)
                wait(pe, S("d_o_out"), g.n)
                nc.tensor.matmul(dO[0:w, 0:r * D], ones96[:, 0:w], bsplit[:, 1:1 + r, :].rearrange("p a d -> p (a d)"),
                                 start=True, stop=False)
                for k in range(r):
                    last = nc.tensor.matmul(dO[0:w, k * D:(k + 1) * D], dhT[:, k * w:(k + 1) * w], W2s[:, :],
                                            start=False, stop=(k == r - 1))
                last.then_inc(S("d_o"), 1)

        def dense_act(act, g, stg):
            w, r = g.p, g.r
            if stg == "T_out":
                act.wait_ge(S("d_xT"), g.n + 1)
                wait(act, S("d_h"), g.n)
                nc.scalar.activation(drT[:, 0:r * w], dX[:, 0:r * w], ACT.Identity, scale=eps1[:, 0:1]
                                     ).then_inc(S("d_xT_out"), 1)
            if stg == "H_out":
                act.wait_ge(S("d_h"), g.n + 1)
                wait(act, S("d_o"), g.n)
                nc.scalar.activation(dhT[:, 0:r * w], dH[:, 0:r * w], ACT.Relu, bias=b1c[:, 0:1]
                                     ).then_inc(S("d_h_out"), 1)
            s = g.slot
            if stg == "sd1":
                act.wait_ge(S("d_var1"), g.n + 1)
                nc.scalar.activation(dsd[0:w, s, 0:r], dmv[0:w, s, 0:r, 1], ACT.Sqrt, bias=epsc[0:w, 0:1]
                                     ).then_inc(S("d_sd1"), 1)
            if stg == "sd2":
                act.wait_ge(S("d_var2"), g.n + 1)
                nc.scalar.activation(dsd2[0:w, s, 0:r], dmv2[0:w, s, 0:r, 1], ACT.Sqrt, bias=epsc[0:w, 0:1]
                                     ).then_inc(S("d_sd2"), 1)
            if stg == "norm":
                act.wait_ge(S("d_shift"), g.n + 1)
                for k in range(r):
                    row = zout[0:w, s, k * D:(k + 1) * D]
                    last = nc.scalar.activation(row, row, ACT.Identity, scale=drs2[0:w, s, k:k + 1],
                                                bias=dshift[0:w, s, k:k + 1])
                last.then_inc(S("d_z"), 1)

        def dense_dve(dve, g, stg):
            w, r, s = g.p, g.r, g.slot
            if stg == "add":
                dve.wait_ge(S("d_o"), g.n + 1)
                nc.vector.tensor_tensor(xin[0:w, s, 0:r * D], dO[0:w, 0:r * D], xin[0:w, s, 0:r * D], ALU.add
                                        ).then_inc(S("d_o_out"), 1)
            if stg == "stats1":
                dve.wait_ge(S("d_o_out"), g.n + 1)
                for k in range(r):
                    last = nc.vector.bn_stats(dst1[0:w, s, k, :], xin[0:w, s, k * D:(k + 1) * D])
                last.then_inc(S("d_st1"), 1)
            if stg == "var1":
                dve.wait_ge(S("d_st1"), g.n + 1)
                take_waits(dve)
                for k in range(r):
                    last = nc.vector.bn_aggr(dmv[0:w, s, k, :], dst1[0:w, s, k, :])
                last.then_inc(S("d_var1"), 1)
            if stg == "rsd1":
                dve.wait_ge(S("d_sd1"), g.n + 1)
                nc.vector.reciprocal(drs[0:w, s, 0:r], dsd[0:w, s, 0:r]).then_inc(S("d_rs1"), 1)
            if stg == "y":
                dve.wait_ge(S("d_rs1"), g.n + 1)
                wait(dve, d_out[s], g.uses * 16)
                for k in range(r):
                    last = nc.vector.scalar_tensor_tensor(zout[0:w, s, k * D:(k + 1) * D],
                                                          xin[0:w, s, k * D:(k + 1) * D], drs[0:w, s, k:k + 1],
                                                          relu_cb[0:w, 2, :], ALU.mult, ALU.add)
                last.then_inc(S("d_y"), 1)
            if stg == "stats2":
                dve.wait_ge(S("d_y"), g.n + 1)
                for k in range(r):
                    last = nc.vector.bn_stats(dst2[0:w, s, k, :], zout[0:w, s, k * D:(k + 1) * D])
                last.then_inc(S("d_st2"), 1)
            if stg == "var2":
                dve.wait_ge(S("d_st2"), g.n + 1)
                take_waits(dve)
                for k in range(r):
                    last = nc.vector.bn_aggr(dmv2[0:w, s, k, :], dst2[0:w, s, k, :])
                last.then_inc(S("d_var2"), 1)
            if stg == "rsd2":
                dve.wait_ge(S("d_sd2"), g.n + 1)
                nc.vector.reciprocal(drs2[0:w, s, 0:r], dsd2[0:w, s, 0:r]).then_inc(S("d_rs2"), 1)
            if stg == "shift":
                dve.wait_ge(S("d_rs2"), g.n + 1)
                nc.vector.scalar_tensor_tensor(dshift[0:w, s, 0:r], dmv2[0:w, s, 0:r, 0], -1.0, drs2[0:w, s, 0:r],
                                               ALU.mult, ALU.mult).then_inc(S("d_shift"), 1)

        def dense_sp(sp, g, stg, free):
            if stg == "load":
                wait(sp, S("d_y"), free)
                sp.dma_start(xin[0:g.p, g.slot, 0:g.r * D], g.dram(x)).then_inc(d_in[g.slot], 16)
            if stg == "store":
                sp.wait_ge(S("d_z"), g.n + 1)
                sp.dma_start(g.dram(out), zout[0:g.p, g.slot, 0:g.r * D]).then_inc(d_out[g.slot], 16)

        def edge_pe(pe, i, k, stg):
            n, b, c = step(i, k), k % 2, k % RING
            if stg == "T":
                pe.wait_ge(gat[k], gathered("edge", i))
                wait(pe, S("e_x_out"), n)
                nc.tensor.transpose(pX[:, 0:P], gx[:, k, 0, :], ident[:, :])
                nc.tensor.transpose(pX[:, P:2 * P], gx[:, k, 1, :], ident[:, :]).then_inc(S("e_x"), 1)
            if stg == "M":
                pe.wait_ge(S("e_x_out"), n + 1)
                wait(pe, S("e_m_out"), n)
                nc.tensor.matmul(pM[:, 0:D], ones96[:, :], bsplit[:, 0, :], start=True, stop=False)
                nc.tensor.matmul(pM[:, 0:D], xT[:, c, 0:P], Wa[:, :], start=False, stop=False)
                nc.tensor.matmul(pM[:, 0:D], xT[:, c, P:2 * P], Wb[:, :], start=False, stop=True
                                 ).then_inc(S("e_m"), 1)
            if stg == "N":
                pe.wait_ge(S("e_m_out"), n + 1)
                wait(pe, S("e_n_out"), n)
                nc.tensor.matmul(pS[:, 0:P], msg[:, b, :], same[:, ds(n * P, P)], start=True, stop=True
                                 ).then_inc(S("e_n"), 1)
            if stg == "H":
                pe.wait_ge(S("e_r"), n + 1)
                wait(pe, S("e_h_out"), n)
                nc.tensor.matmul(pH[:, 0:2 * P], W1s[:, :], rT[:, c, :], start=True, stop=True).then_inc(S("e_h"), 1)
            if stg == "O":
                pe.wait_ge(S("e_h_out"), n + 1)
                wait_tile(pe, "e_o_out", i, k - 1)
                nc.tensor.matmul(pO[:, 0:2 * D], ones96[:, :], bsplit[:, 1:3, :].rearrange("p a d -> p (a d)"),
                                 start=True, stop=False)
                for a in range(2):
                    last = nc.tensor.matmul(pO[:, a * D:(a + 1) * D], hT[:, b, a * P:(a + 1) * P], W2s[:, :],
                                            start=False, stop=(a == 1))
                last.then_inc(S("e_o"), 1)

        def edge_act(act, i, k, stg):
            n, b, c = step(i, k), k % 2, k % RING
            if stg == "T_out":
                act.wait_ge(S("e_x"), n + 1)
                wait(act, S("e_h"), n - (RING - 1))
                nc.scalar.copy(xT[:, c, :], pX[:, 0:2 * P])
                nc.scalar.activation(rT[:, c, 0:P], pX[:, 0:P], ACT.Identity, scale=eps1[:, 0:1]
                                     ).then_inc(S("e_x_out"), 1)
            if stg == "M_out":
                act.wait_ge(S("e_m"), n + 1)
                wait(act, S("e_n"), n - 1)
                nc.scalar.activation(msg[:, b, :], pM[:, 0:D], ACT.Relu).then_inc(S("e_m_out"), 1)
            if stg == "H_out":
                act.wait_ge(S("e_h"), n + 1)
                wait(act, S("e_o"), n - 1)
                nc.scalar.activation(hT[:, b, :], pH[:, 0:2 * P], ACT.Relu, bias=b1c[:, 0:1]).then_inc(S("e_h_out"), 1)
            if stg == "sd":
                act.wait_ge(S("e_var"), n + 1)
                nc.scalar.activation(sd[:, c, :], mv[:, c, :, 1], ACT.Sqrt, bias=epsc[:, 0:1]).then_inc(S("e_sd"), 1)
            if stg == "norm":
                slot = k % STORES
                act.wait_ge(S("e_shift"), n + 1)
                wait(act, stored[slot], stored_before("edge", i, k))
                for a in range(2):
                    last = nc.scalar.activation(yo[:, slot, a, :], res[:, c, a, :], ACT.Identity,
                                                scale=rs[:, c, a:a + 1], bias=shift[:, c, a:a + 1])
                last.then_inc(S("e_y"), 1)

        def edge_dve(dve, i, k, stg):
            n, b, c = step(i, k), k % 2, k % RING
            if stg == "N_out":
                dve.wait_ge(S("e_n"), n + 1)
                wait(dve, S("e_n_out"), n)
                wait(dve, S("e_r"), n - 1)
                nc.vector.scalar_tensor_tensor(aggT[:, b, :], cont[:, ds(n * P, P)], aggT[:, 1 - b, P - 1:P],
                                               pS[:, 0:P], ALU.mult, ALU.add).then_inc(S("e_n_out"), 1)
            if stg == "in":
                dve.wait_ge(S("e_n_out"), n + 1)
                nc.vector.scalar_tensor_tensor(rT[:, c, P:2 * P], xT[:, c, P:2 * P], eps1[:, 0:1], aggT[:, b, :],
                                               ALU.mult, ALU.add).then_inc(S("e_r"), 1)
            if stg == "add":
                dve.wait_ge(S("e_o"), n + 1)
                wait(dve, S("e_y"), n - (RING - 1))
                nc.vector.tensor_tensor(res[:, c, :, :].rearrange("p a d -> p (a d)"), pO[:, 0:2 * D],
                                        gx[:, k, :, :].rearrange("p a d -> p (a d)"), ALU.add
                                        ).then_inc(half_sem("e_o_out", k), 1)
            if stg == "stats":
                wait_tile(dve, "e_o_out", i, k)
                for a in range(2):
                    last = nc.vector.bn_stats(st[:, c, a, :], res[:, c, a, :])
                last.then_inc(S("e_st"), 1)
            if stg == "var":
                dve.wait_ge(S("e_st"), n + 1)
                take_waits(dve)
                for a in range(2):
                    last = nc.vector.bn_aggr(mv[:, c, a, :], st[:, c, a, :])
                last.then_inc(S("e_var"), 1)
            if stg == "rsd":
                dve.wait_ge(S("e_sd"), n + 1)
                nc.vector.reciprocal(rs[:, c, :], sd[:, c, :]).then_inc(S("e_rs"), 1)
            if stg == "shift":
                dve.wait_ge(S("e_rs"), n + 1)
                nc.vector.scalar_tensor_tensor(shift[:, c, :], mv[:, c, :, 0], -1.0, rs[:, c, :], ALU.mult, ALU.mult
                                               ).then_inc(S("e_shift"), 1)

        def edge_sp(sp, i, k, stg):
            n = step(i, k)
            if stg == "store":
                sp.wait_ge(S("e_y"), n + 1)
                sp.dma_start(y_dram[ds(n * (2 * P), 2 * P), :].rearrange("(p a) d -> p (a d)", a=2),
                             yo[:, k % STORES, :, :].rearrange("p a d -> p (a d)")
                             ).then_inc(stored[k % STORES], 16)

        def conv_pe(pe, c, i, k, stg):
            q, n, b = f"conv{c}", step(i, k), k % 2
            m = n + (c - 1) * T
            if stg == "A":
                pe.wait_ge(gat[k], gathered(q, i))
                if c == 1:
                    pe.wait_ge(S("c1_scaled"), n + 1)
                wait(pe, S("c_a_out"), m - 1)
                nc.tensor.matmul((pX, pS)[b][:, 0:P], gx[:, k, 0, :], same[:, ds(n * P, P)], start=True, stop=True
                                 ).then_inc(half_sem("c_a", k), 1)
            if stg == "B":
                pe.wait_ge(S("c_a_out"), m + 1)
                if c < 3:
                    wait(pe, S("c_u"), m - 1)
                else:
                    pe.wait_ge(S("c_u"), 2 * T)
                    wait_tile(pe, "c3_r", i, k - 2)
                nc.tensor.matmul((pM, pH)[b][:, 0:D], ones96[:, :], bsplit[:, 4 + c, :], start=True, stop=False)
                nc.tensor.matmul((pM, pH)[b][:, 0:D], aggT[:, b, :], Cs[c - 1][:, :], start=False, stop=True
                                 ).then_inc(S("c_b"), 1)

        def conv_dve(dve, c, i, k, stg):
            n, b = step(i, k), k % 2
            m = n + (c - 1) * T
            if stg == "A_out":
                wait_tile(dve, "c_a", i + (c - 1) * TURNS, k)
                wait(dve, S("c_b"), m - 1)
                wait(dve, S("c_a_out"), m)
                nc.vector.scalar_tensor_tensor(aggT[:, b, :], cont[:, ds(n * P, P)], aggT[:, 1 - b, P - 1:P],
                                               (pX, pS)[b][:, 0:P], ALU.mult, ALU.add).then_inc(S("c_a_out"), 1)
            if c == 3:
                r = k % RING
                if stg == "add":
                    dve.wait_ge(S("c_b"), m + 1)
                    dve.wait_ge(yd_in[k // HALF], i * (16 * HALF) + 16 * HALF)
                    wait(dve, S("c3_z"), n - (RING - 1))
                    nc.vector.scalar_tensor_tensor(res[:, r, 0, :], (pM, pH)[b][:, 0:D], 0.0, yd[:, k, :], ALU.max, ALU.add
                                                   ).then_inc(half_sem("c3_r", k), 1)
                if stg == "stats":
                    wait_tile(dve, "c3_r", i, k)
                    nc.vector.bn_stats(st[:, r, 0, :], res[:, r, 0, :]).then_inc(S("c3_st"), 1)
                if stg == "var":
                    dve.wait_ge(S("c3_st"), n + 1)
                    take_waits(dve)
                    nc.vector.bn_aggr(mv[:, r, 0, :], st[:, r, 0, :]).then_inc(S("c3_var"), 1)
                if stg == "rsd":
                    dve.wait_ge(S("c3_sd"), n + 1)
                    nc.vector.reciprocal(rs[:, r, 0:1], sd[:, r, 0:1]).then_inc(S("c3_rs"), 1)
                if stg == "shift":
                    dve.wait_ge(S("c3_rs"), n + 1)
                    nc.vector.scalar_tensor_tensor(shift[:, r, 0:1], mv[:, r, 0, 0:1], -1.0, rs[:, r, 0:1],
                                                   ALU.mult, ALU.mult).then_inc(S("c3_shift"), 1)

        def conv_act(act, c, i, k, stg):
            n, b = step(i, k), k % 2
            m = n + (c - 1) * T
            if stg == "scale" and c == 1:
                nc.scalar.activation(same[:, ds(n * P, P)], same[:, ds(n * P, P)], ACT.Identity,
                                     scale=scale[:, ds(n, 1)]).then_inc(S("c1_scaled"), 1)
            if stg == "relu" and c < 3:
                slot = k % STORES
                act.wait_ge(S("c_b"), m + 1)
                act.wait_ge(stored[slot], stored_before(f"conv{c}", i, k))
                nc.scalar.activation(uo[:, slot, :], (pM, pH)[b][:, 0:D], ACT.Relu).then_inc(S("c_u"), 1)
            if c == 3:
                r = k % RING
                if stg == "sd":
                    act.wait_ge(S("c3_var"), n + 1)
                    nc.scalar.activation(sd[:, r, 0:1], mv[:, r, 0, 1:2], ACT.Sqrt, bias=epsc[:, 0:1]
                                         ).then_inc(S("c3_sd"), 1)
                if stg == "norm":
                    act.wait_ge(S("c3_shift"), n + 1)
                    nc.scalar.activation(gz[:, k, :], res[:, r, 0, :], ACT.Identity, scale=rs[:, r, 0:1],
                                         bias=shift[:, r, 0:1]).then_inc(S("c3_z"), 1)

        def conv_sp(sp, c, i, k, stg):
            n = step(i, k)
            m = n + (c - 1) * T
            if stg == "store" and c < 3:
                sp.wait_ge(S("c_u"), m + 1)
                sp.dma_start(u_dram[c - 1][ds(n * P, P), :], uo[:, k % STORES, :]
                             ).then_inc(stored[k % STORES], 16)

        def run(eng, count, turn):
            turn(0)
            with eng.Fori(1, count) as i:
                turn(i)

        def run_pairs(eng, turn):
            turn(0, 0)
            with eng.Fori(1, (TURNS + 1) // 2) as i:
                turn(i * 2 - 1, 1)
                turn(i * 2, 0)

        def lag(k):
            return (LOOKS if k >= LOOKS else k + BODY - max(q for q in range(BODY) if q % LOOKS == k)) - 1

        def phase_loop(eng, phase, tile_fn, dense_fn):
            stages = {"edge": EDGE, "conv1": CONV, "conv2": CONV, "conv3": CONV3}[phase]
            groups = SPREAD.get(phase, 0)
            late_first = sorted(stages.items(), key=lambda kv: -kv[1])
            dense_late_first = sorted(DENSE.get(phase, {}).items(), key=lambda kv: -kv[1])

            def steps(i, has_tiles, has_before):
                for t in range(BODY):
                    for second in (False, True):
                        for stg, off in late_first:
                            if (stg in SECOND) == second:
                                if t >= off and has_tiles:
                                    tile_fn(i, t - off, stg)
                                if t < off and has_before:
                                    tile_fn(i - 1, t - off + BODY, stg)
                        for j in reversed(range(groups)):
                            for stg, off in dense_late_first:
                                due = j * BODY // groups + off
                                if (stg in SECOND) == second and due == t and has_tiles:
                                    dense_fn(looped_group(phase, i, j), stg, i, j)
                                if (stg in SECOND) == second and due % BODY == t and due >= BODY and has_before:
                                    dense_fn(looped_group(phase, i - 1, j), stg, i - 1, j)

            steps(0, True, False)
            with eng.Fori(1, TURNS) as i:
                steps(i, True, True)
            steps(TURNS, False, True)

        def ahead(dense_fn):
            for t in range(2 * AHEAD + max(DENSE["edge"].values()) + 1):
                for m in range(AHEAD + 1):
                    for stg, off in DENSE["edge"].items():
                        if 2 * m + off == t:
                            dense_fn(ahead_group(m), stg)

        def free_after(phase, i, j):
            n = looped_group(phase, i, j).n
            if not isinstance(i, int):
                return n - (SPREAD[phase] - 1)
            if i > 0:
                return n - (SPREAD[phase] - 1)
            return n - j

        block = ctx.enter_context(nc.Block())

        @block.sync
        def _(sp):
            sp.wait_ge(s_pad, 1)
            for a, v in ((0, src), (1, dst)):
                sp.dma_start(rows_i[0:FULL, a, :], v[0:FULL * P].rearrange("(t p) -> t p", p=P)).then_inc(s_rows, 16)
                sp.dma_start(rows_i[FULL:FULL + 1, a, 0:E - FULL * P],
                             v[FULL * P:E].rearrange("(t p) -> t p", t=1)).then_inc(s_rows, 16)
            for tile_, w in ((Wa, W_edge[0:D, :]), (Wb, W_edge[D:2 * D, :]), (W1s, W1), (W2s, W2),
                             (Cs[0], C1), (Cs[1], C2), (Cs[2], C3)):
                sp.dma_start(tile_[:, :], w).then_inc(s_w, 16)
            sp.dma_start(b1c[:, :], b1.rearrange("(p a) -> p a", a=1)).then_inc(s_w, 16)
            sp.dma_start(eps1[:, :], eps.rearrange("(p a) -> p a", a=1).to_broadcast([P, 1])).then_inc(s_w, 16)
            for a, v in enumerate((c1, c2, c3)):
                sp.dma_start(cb[:, a, :], v.rearrange("(a d) -> a d", a=1).to_broadcast([P, D])).then_inc(s_w, 16)
            for a, v in enumerate((b_edge, b2, c1, c2, c3)):
                sp.dma_start(braw[:, a, :], v.rearrange("(a d) -> a d", a=1).to_broadcast([96, D])).then_inc(s_w, 16)
            sp.wait_ge(s_padded, 1)
            for a in range(2):
                sp.dma_start(ids_dram[a, 1:1 + EP].rearrange("(t p) -> t p", p=P), rows[:, a, :]).then_inc(s_ids, 16)
            sp.dma_start(ids_dram[1:2, 0:1], part[0:1, 0:1]).then_inc(s_ids, 16)
            sp.dma_start(ids_dram[1:2, EP + 1:EP + 2], part[0:1, 2:3]).then_inc(s_ids, 16)
            sp.wait_ge(s_ids, 16 * 4)
            sp.dma_start(rows[:, 3, :], ids_dram[1, 2:2 + EP].rearrange("(t p) -> t p", p=P)).then_inc(s_srt, 16)
            sp.dma_start(srt[:, 0, 0:1], ids_dram[1, 0:EP].rearrange("(t p) -> t p", p=P)[:, 0:1]).then_inc(s_srt, 16)
            sp.dma_start(srt[:, 0, 1:1 + P], ids_dram[1, 1:1 + EP].rearrange("(t p) -> t p", p=P)).then_inc(s_srt, 16)
            sp.dma_start(srt[1:T, 1, 0:1], ids_dram[1, 0:EP - P].rearrange("(t p) -> t p", p=P)[:, 0:1]).then_inc(s_srt, 16)
            sp.dma_start(srt[1:T, 1, 1:1 + P], ids_dram[1, 1:1 + EP - P].rearrange("(t p) -> t p", p=P)).then_inc(s_srt, 16)
            def spread_ids(i, a):
                wait(sp, s_bcused, i - 1)
                for v, ids_bc, w in ((0, src_bc[a], T), (1, dst_bc[a], P)):
                    sp.dma_start(ids_bc, ids_dram[v:v + 1, ds(i * CH + 1, CH)].to_broadcast([w, CH])
                                 ).then_inc(s_bc[a], 16)
            spread_ids(0, 0)
            sp.wait_ge(s_ci, 1)
            for a in range(2):
                sp.dma_start(u_dram[a][EP:EP + 1, :], relu_cb[0:1, a, :]).then_inc(s_const_u, 16)
            sp.wait_ge(S("v_tab"), 1)
            for a in range(2):
                sp.dma_start(count_dram[a * T * LO:(a + 1) * T * LO, :].rearrange("(p l) o -> p (l o)", l=LO),
                             tab[:, a * LO:(a + 1) * LO]).then_inc(s_table, 16)

            with sp.Fori(1, (TURNS + 1) // 2) as i:
                spread_ids(i * 2 - 1, 1)
                spread_ids(i * 2, 0)
            ahead(lambda g, stg: dense_sp(sp, g, stg, g.n - SLOTS + 1))
            phase_loop(sp, "edge", lambda i, k, stg: edge_sp(sp, i, k, stg),
                       lambda g, stg, i, j: dense_sp(sp, g, stg, free_after("edge", i, j)))
            for c in (1, 2):
                phase_loop(sp, f"conv{c}", lambda i, k, stg: conv_sp(sp, c, i, k, stg),
                           lambda g, stg, i, j: dense_sp(sp, g, stg, free_after(f"conv{c}", i, j)))

            def load_y(i):
                for k in range(BODY):
                    n = step(i, k)
                    if k % HALF == 0:
                        wait(sp, half_sem("c3_r", k), i * HALF)
                    sp.dma_start(yd[:, k, :], y_dram[ds(n * (2 * P), 2 * P), :].rearrange(
                        "(p a) d -> p a d", a=2)[:, 1, :]).then_inc(yd_in[k // HALF], 16)
            run(sp, TURNS, load_y)
            for k in range(BODY):
                sp.wait_ge(gat[k], gathered("conv3", TURNS - 1) + 16)

        @block.gpsimd
        def _(pool):
            nc.gpsimd.memset(rows_i[:, 0, :], SRC_PAD)
            nc.gpsimd.memset(rows_i[:, 1, :], DST_PAD).then_inc(S("g_m"), 1)
            nc.gpsimd.memset(ident[:, :], 0.0)
            nc.gpsimd.memset(first_row[:, :], 1.0)
            nc.gpsimd.memset(last_row[:, :], 1.0).then_inc(S("g_z"), 1)
            nc.gpsimd.iota(enum_i[:, :], [[P, T]], base=0, channel_multiplier=1)
            nc.gpsimd.iota(ramp_i[:, :], [[1, LO]], base=0, channel_multiplier=0)
            nc.gpsimd.iota(part_i[:, :], [[0, 1]], base=0, channel_multiplier=1).then_inc(s_iota, 1)
            pool.wait_ge(S("g_z"), 1)
            pool.wait_ge(S("g_m"), 1)
            nc.gpsimd.affine_select(out=ident[:, :], in_=ident[:, :], compare_op=ALU.not_equal, fill=1.0, base=0,
                                    pattern=[[-1, P]], channel_multiplier=1).then_inc(s_pad, 1)
            nc.gpsimd.affine_select(out=last_row[:, :], in_=last_row[:, :], compare_op=ALU.is_ge, fill=0.0,
                                    base=-(P - 1), pattern=[[0, P]], channel_multiplier=1).then_inc(s_iota, 1)
            nc.gpsimd.affine_select(out=first_row[:, :], in_=first_row[:, :], compare_op=ALU.is_ge, fill=0.0,
                                    base=0, pattern=[[0, P]], channel_multiplier=-1).then_inc(s_iota, 1)
            pool.wait_ge(S("v_runs"), 1)
            nc.gpsimd.affine_select(out=runs[:, 0, :], in_=runs[:, 0, :], compare_op=ALU.is_ge, fill=0.0, base=0,
                                    pattern=[[1, T]], channel_multiplier=-1)
            nc.gpsimd.affine_select(out=runs[:, 1, :], in_=runs[:, 1, :], compare_op=ALU.is_ge, fill=0.0, base=0,
                                    pattern=[[-1, T]], channel_multiplier=1).then_inc(S("g_runs"), 1)

            def halves(h):
                return range(h * HALF, (h + 1) * HALF)

            def take_indices(to, column, i, h, signal, count):
                take_waits(pool)
                nc.gpsimd.tensor_copy(to[:, h * HALF:(h + 1) * HALF], idx[:, column, ds(i * BODY + h * HALF, HALF)]
                                      ).then_inc(signal, 1)
                pool.wait_ge(signal, count)
                take_waits(pool)

            def gather(to, table, index):
                return nc.gpsimd.indirect_dma_start(to, None, table, bass.IndirectOffsetOnAxis(ap=index, axis=0))

            def edge_gathers(i):
                for h in range(2):
                    wait(pool, S("e_x_out"), i * BODY - BODY + (h + 1) * HALF)
                    take_indices(stage[:, 1, :], DST_I, i, h, S("g_dst"), i * 2 + h + 1)
                    take_indices(stage[:, 0, :], SRC_I, i, h, S("g_src"), i * 2 + h + 1)
                    for k in halves(h):
                        if not isinstance(i, int):
                            wait_tile(pool, "e_o_out", i - 1, k)
                            take_waits(pool)
                        gather(gx[:, k, 0, :], x, stage[:, 0, k:k + 1]).then_inc(gat[k], 16)
                        gather(gx[:, k, 1, :], x, stage[:, 1, k:k + 1]).then_inc(gat[k], 16)

            def conv_indices(c, i, h):
                wait(pool, S(f"c_a_{h}"), i * HALF + (c - 1) * (TURNS * HALF))
                take_indices(stage[:, 0, :], Y_I if c == 1 else U_I, i, h, S("g_row"), (i + (c - 1) * TURNS) * 2 + h + 1)

            def conv_gather(c, k):
                gather(gx[:, k, 0, :], (y_dram, u_dram[0], u_dram[1])[c - 1], stage[:, 0, k:k + 1]).then_inc(gat[k], 16)

            def conv_gathers(c, i, h):
                conv_indices(c, i, h)
                for k in halves(h):
                    conv_gather(c, k)

            def scatter(i, k):
                if k % HALF == 0:
                    h = k // HALF
                    for kk in halves(h):
                        pool.wait_ge(gat[kk], gathered("conv3", i))
                    take_indices(ostage, O_I, i, h, S("g_out"), i * 2 + h + 1)
                pool.wait_ge(S("c3_z"), i * BODY + (k + 1))
                take_waits(pool)
                nc.gpsimd.indirect_dma_start(
                    out, bass.IndirectOffsetOnAxis(ap=ostage[:, k:k + 1], axis=0), gz[:, k, :], None,
                    bounds_check=N - 1, oob_is_err=False).then_inc(gat[k], 16)

            pool.wait_ge(S("v_idx"), 1)
            edge_gathers(0)

            def take_counts(i, h):
                pool.wait_ge(s_counts[h], i * (16 * HALF) + 16 * HALF)
                take_waits(pool)
                nc.gpsimd.tensor_copy(deg_out[:, ds(i * BODY + h * HALF, HALF)], deg_in_flight[:, h * HALF:(h + 1) * HALF]
                                      ).then_inc(S("g_counted"), 1)

            def count_gathers(i):
                for h in range(2):
                    if not isinstance(i, int) or i > 0:
                        take_counts(i - 1, h)
                        pool.wait_ge(S("g_counted"), i * 2 + h - 1)
                    take_indices(stage[:, 2, :], SRC_I, i, h, S("g_cnt"), i * 2 + h + 1)
                    for k in halves(h):
                        gather(deg_in_flight[:, k:k + 1], count_dram, stage[:, 2, k:k + 1]).then_inc(s_counts[h], 16)
            pool.wait_ge(s_table, 32)
            run(pool, COUNTED, count_gathers)
            with pool.Fori(1, TURNS - COUNTED + 1) as i:
                edge_gathers(i)
                count_gathers(i + (COUNTED - 1))
            with pool.Fori(TURNS - COUNTED + 1, TURNS) as i:
                edge_gathers(i)
            for h in range(2):
                take_counts(TURNS - 1, h)
            all_stored(pool, "edge")
            pool.wait_ge(S("v_rowidx"), 1)
            run(pool, TURNS, lambda i: (conv_gathers(1, i, 0), conv_gathers(1, i, 1)))
            all_stored(pool, "conv1")
            pool.wait_ge(s_const_u, 32)
            run(pool, TURNS, lambda i: (conv_gathers(2, i, 0), conv_gathers(2, i, 1)))
            all_stored(pool, "conv2")
            for j in range(SLOTS):
                pool.wait_ge(d_out[j], 16 * (len(range(j, AHEAD + 1, SLOTS)) + turns_of_slot(PHASES[:3], j)))

            def last_turn(i, has_tiles, has_before):
                for k in range(BODY):
                    if has_tiles:
                        if k % HALF == 0:
                            conv_indices(3, i, k // HALF)
                        conv_gather(3, k)
                    if k >= LAG and has_tiles:
                        scatter(i, k - LAG)
                    if k < LAG and has_before:
                        scatter(i - 1, k - LAG + BODY)
            last_turn(0, True, False)
            with pool.Fori(1, TURNS) as i:
                last_turn(i, True, True)
            last_turn(TURNS, False, True)

        @block.vector
        def _(dve):
            count = [0]

            def link(ins):
                count[0] += 1
                ins.then_inc(s_v, 1)
                dve.wait_ge(s_v, count[0])

            V = nc.vector
            V.memset(zeros[:, :], 0.0)
            V.memset(ones96[:, :], 0.0)
            V.memset(bsplit[:, :, :], 0.0)
            V.memset(epsc[:, :], EPS)
            V.memset(aggT[:, :, :], 0.0)
            V.memset(srt[:, :, :], 0.0)
            link(V.memset(part[:, 2:3], float(DST_END)))
            for q in range(3):
                V.memset(ones96[32 * q:32 * q + 1, :], 1.0)
            dve.wait_ge(s_iota, 3)
            V.tensor_copy(enum[:, :], enum_i[:, :])
            V.tensor_copy(ramp[:, :], ramp_i[:, :])
            link(V.memset(part[:, 0:1], -1.0))
            link(V.tensor_copy(part[:, 1:2], part_i[:, :]))
            dve.wait_ge(s_rows, 64)
            V.tensor_copy(rows[:, 0, :], rows_i[:, 0, :])
            V.tensor_copy(rows[:, 1, :], rows_i[:, 1, :])
            link(V.tensor_scalar(tmp_i[:, :], rows_i[:, 0, :], 8, None, ALU.logical_shift_right))
            V.tensor_copy(rows[:, 2, :], tmp_i[:, :]).then_inc(s_padded, 1)
            dve.wait_ge(s_padded, 1)
            dve.wait_ge(s_pe, 1)
            link(V.tensor_copy(cols[:, 0:3, :], pX[:, 0:3 * T].rearrange("p (a t) -> p a t", a=3)))
            V.scalar_tensor_tensor(cols[:, 3, :], cols[:, 2, :], -float(LO), cols[:, 0, :], ALU.mult, ALU.add)
            V.tensor_scalar(idx[:, SRC_I, :], cols[:, 0, :], float(N - 1), None, ALU.min)
            link(V.tensor_scalar(idx[:, DST_I, :], cols[:, 1, :], float(N - 1), None, ALU.min))
            V.tensor_scalar(reach[:, :], cols[:, 0, :], float(LO - 1), 1.0, ALU.mult, ALU.add)
            V.memset(first_bc[:, 0:1], -1.0).then_inc(S("v_idx"), 1)
            dve.wait_ge(s_pe, 2)
            link(V.tensor_copy(first_bc[:, 1:T], pM[:, 0:T - 1]))
            V.tensor_copy(next_bc[:, 0:T - 1], pM[:, T + 1:2 * T])
            V.memset(next_bc[:, T - 1:T], -2.0)
            V.tensor_scalar(runs[:, 0, :], pM[0:T, 0:T], rows[:, 1, P - 1:P], None, ALU.is_equal)
            V.tensor_scalar(runs[:, 1, :], pM[0:T, T:2 * T], rows[:, 1, 0:1], None, ALU.is_equal
                            ).then_inc(S("v_runs"), 1)
            def one_hot(i):
                for b in range(RING):
                    wait(dve, s_hist, i * RING + (b - RING + 1))
                    V.tensor_scalar(hot_hi[:, b, :], ramp[:, 0:HI], cols[:, 2, ds(i * RING + b, 1)], None, ALU.is_equal)
                    V.tensor_scalar(hot_lo[:, b, :], ramp[:, :], cols[:, 3, ds(i * RING + b, 1)], None, ALU.is_equal
                                    ).then_inc(s_hot, 1)
            run(dve, T // RING, one_hot)
            dve.wait_ge(s_pe, 3)
            V.tensor_copy(tab[:, :], pH[0:T, :]).then_inc(S("v_tab"), 1)
            dve.wait_ge(s_srt, 80)
            dve.wait_ge(s_pe, 4)
            link(V.tensor_copy(cols[:, 4, :], pX[:, 3 * T:4 * T]))
            link(V.tensor_tensor(fidx[:, 0, :], cols[:, 1, :], cols[:, 4, :], ALU.is_equal))
            link(V.scalar_tensor_tensor(idx[:, O_I, :], fidx[:, 0, :], 65536.0, cols[:, 1, :], ALU.mult, ALU.add))
            V.tensor_copy(before[:, :], srt[:, 0, 0:1])
            link(V.tensor_scalar(srt[:, 0, P + 1:P + 2], part[0:T, 1:2], float(P * LO), None, ALU.mult))
            link(V.tensor_scalar(srt[:, 1, P + 1:P + 2], srt[:, 0, P + 1:P + 2], -float(P * LO), 0.0,
                                 ALU.add, ALU.max))
            link(V.tensor_tensor(srt[:, 0, :], srt[:, 0, :], srt[:, 1, :], ALU.subtract))
            link(V.tensor_copy(srt_i[:, :], srt[:, 0, :]))
            link(V.tensor_scalar(srt_i[:, :], srt_i[:, :], 255, None, ALU.bitwise_and))
            link(V.tensor_copy(step_lo[:, :], srt_i[:, :]))
            link(V.tensor_tensor(step_hi[:, :], srt[:, 0, :], step_lo[:, :], ALU.subtract))
            dve.wait_ge(s_w, 16 * 17)
            link(V.tensor_scalar(eps1[:, :], eps1[:, :], 1.0, None, ALU.add))
            V.tensor_scalar(relu_cb[:, :, :], cb[:, :, :], 0.0, None, ALU.max).then_inc(s_ci, 1)
            link(V.tensor_copy(bhalf[:, :, :], braw[:, :, :]))
            for q in range(3):
                r_ = slice(32 * q, 32 * q + 1)
                V.tensor_copy(bsplit[r_, 0, :], bhalf[r_, 0, :])
                V.tensor_copy(bsplit[r_, 5:8, :], bhalf[r_, 2:5, :])
                link(V.tensor_copy(bsplit[r_, 1:5, :], bhalf[r_, 1, :].unsqueeze(1).to_broadcast([1, 4, D])))
                if q < 2:
                    link(V.tensor_tensor(braw[:, :, :], braw[:, :, :], bhalf[:, :, :], ALU.subtract))
                    link(V.tensor_copy(bhalf[:, :, :], braw[:, :, :]))
            V.memset(mark[:, :], 0.0).then_inc(S("v_bias"), 1)

            def chunk(i, a):
                dve.wait_ge(s_bc[a], i * 16 + (32 - 16 * a))
                wait(dve, s_look, i * BODY - BODY)
                V.tensor_scalar(above[a][:, :], src_bc[a], before[:, 0:1], None, ALU.is_ge).then_inc(s_hi, 1)
                V.tensor_tensor(cont[:, ds(i * CH, CH)].rearrange("p (t f) -> p t f", f=P),
                                dst_bc[a].rearrange("p (t f) -> p t f", f=P),
                                first_bc[:, ds(i * BODY, BODY)].unsqueeze(2).to_broadcast([P, BODY, P]), ALU.is_equal)
                for k in range(BODY):
                    n, b = step(i, k), k % LOOKS
                    last = V.tensor_scalar(same[:, ds(n * P, P)], dst_bc[a][:, k * P:(k + 1) * P], cols[:, 1, ds(n, 1)],
                                           None, ALU.is_equal, ALU.add, accum_out=own[:, ds(n, 1)])
                    if k == BODY - 1:
                        last.then_inc(s_bcused, 1)
                    dve.wait_ge(S("a_looked"), n + 1)
                    V.tensor_scalar(looked[b], looked[b], float(LO), look_banks[b][:, P + 1:P + 2],
                                    ALU.min, ALU.add, accum_out=found[:, ds(n, 1)]).then_inc(s_looked, 1)
            run_pairs(dve, chunk)
            dve.wait_ge(s_looked, T)
            dve.wait_ge(s_pe, 5)
            V.tensor_copy(ends[:, :, :], pS[0:T, 0:2 * P].rearrange("p (a m) -> p a m", a=2)).then_inc(S("v_ends"), 1)
            dve.wait_ge(s_pe, 6)
            V.tensor_tensor(deg_after[:, :], cols[:, 1, :], next_bc[:, :], ALU.is_equal)
            link(V.tensor_tensor(deg[:, :], cols[:, 1, :], first_bc[:, :], ALU.is_equal))
            V.tensor_tensor(deg_after[:, 0:T - 1], deg_after[:, 0:T - 1], pS[:, 2 * P + T + 1:2 * P + 2 * T], ALU.mult)
            link(V.tensor_tensor(deg[:, 1:T], deg[:, 1:T], pS[:, 2 * P:2 * P + T - 1], ALU.mult))
            link(V.tensor_tensor(deg[:, :], deg[:, :], own[:, :], ALU.add))
            link(V.tensor_tensor(deg[:, :], deg[:, :], deg_after[:, :], ALU.add))
            link(V.tensor_scalar(deg[:, :], deg[:, :], 1.0, None, ALU.max))
            link(V.tensor_copy(found_i[:, 0, :], found[:, :]))
            V.tensor_scalar(found_i[:, 1, :], found_i[:, 0, :], LO - 1, None, ALU.bitwise_and)
            link(V.tensor_scalar(found_i[:, 0, :], found_i[:, 0, :], 8, None, ALU.logical_shift_right))
            V.tensor_copy(below[:, :], found_i[:, 0, :])
            link(V.tensor_copy(equal[:, :], found_i[:, 1, :]))
            link(V.scalar_tensor_tensor(below[:, :], below[:, :], -1.0, equal[:, :], ALU.add, ALU.add))
            link(V.tensor_scalar(hit[:, :], equal[:, :], 1.0, None, ALU.min))
            link(V.tensor_scalar(fidx[:, 1, :], below[:, :], -float(EP + 1), None, ALU.add))
            link(V.tensor_tensor(fidx[:, 1, :], fidx[:, 1, :], hit[:, :], ALU.mult))
            link(V.tensor_scalar(idx[:, U_I, :], fidx[:, 1, :], float(EP), None, ALU.add))
            link(V.tensor_tensor(fidx[:, 0, :], below[:, :], enum[:, :], ALU.subtract))
            link(V.tensor_scalar(fidx[:, 0, :], fidx[:, 0, :], 2.0, -1.0, ALU.mult, ALU.add))
            link(V.tensor_tensor(fidx[:, 0, :], fidx[:, 0, :], hit[:, :], ALU.mult))
            link(V.scalar_tensor_tensor(idx[:, Y_I, :], enum[:, :], 2.0, fidx[:, 0, :], ALU.mult, ALU.add))
            V.memset(mark[:, :], 0.0).then_inc(S("v_rowidx"), 1)

            ahead(lambda g, stg: dense_dve(dve, g, stg))
            phase_loop(dve, "edge", lambda i, k, stg: edge_dve(dve, i, k, stg),
                       lambda g, stg, i, j: dense_dve(dve, g, stg))
            dve.wait_ge(S("g_counted"), 2 * TURNS)
            V.tensor_scalar(deg_out[:, :], deg_out[:, :], 1.0, None, ALU.max).then_inc(S("v_deg"), 1)
            dve.wait_ge(s_root, 1)
            V.reciprocal(deg[:, :], deg[:, :])
            link(V.reciprocal(deg_out[:, :], deg_out[:, :]))
            V.tensor_tensor(scale[:, :], deg[:, :], deg_out[:, :], ALU.mult).then_inc(S("v_scale"), 1)
            for c in (1, 2, 3):
                phase_loop(dve, f"conv{c}", lambda i, k, stg: conv_dve(dve, c, i, k, stg),
                           lambda g, stg, i, j: dense_dve(dve, g, stg))

        @block.scalar
        def _(act):
            act.wait_ge(S("v_idx"), 1)

            def look(i):
                for k in range(BODY):
                    n, b = step(i, k), k % LOOKS
                    act.wait_ge(s_look, n + 1)
                    wait(act, s_looked, n - lag(k))
                    nc.scalar.activation(looked[b], look_banks[b][:, 0:P + 1], ACT.Relu, scale=-float(LO - 1),
                                         bias=reach[:, ds(n, 1)]).then_inc(S("a_looked"), 1)
            run(act, TURNS, look)
            ahead(lambda g, stg: dense_act(act, g, stg))
            phase_loop(act, "edge", lambda i, k, stg: edge_act(act, i, k, stg),
                       lambda g, stg, i, j: dense_act(act, g, stg))
            act.wait_ge(S("v_deg"), 1)
            nc.scalar.activation(deg[:, :], deg[:, :], ACT.Sqrt)
            nc.scalar.activation(deg_out[:, :], deg_out[:, :], ACT.Sqrt).then_inc(s_root, 1)
            act.wait_ge(S("v_scale"), 1)
            for c in (1, 2, 3):
                phase_loop(act, f"conv{c}", lambda i, k, stg: conv_act(act, c, i, k, stg),
                           lambda g, stg, i, j: dense_act(act, g, stg))

        @block.tensor
        def _(pe):
            pe.wait_ge(s_iota, 3)
            pe.wait_ge(s_padded, 1)
            for a in range(3):
                last = nc.tensor.transpose(pX[:, a * T:(a + 1) * T], rows[:, a, :], ident[0:T, 0:T])
            last.then_inc(s_pe, 1)
            pe.wait_ge(S("v_idx"), 1)
            nc.tensor.matmul(pM[:, 0:T], last_row[:, :], cols[:, 1, :], start=True, stop=True)
            nc.tensor.matmul(pM[:, T:2 * T], first_row[:, :], cols[:, 1, :], start=True, stop=True).then_inc(s_pe, 1)
            nc.tensor.matmul(pH[0:T, :], zeros[:, 0:T], zeros[:, :], start=True, stop=False)

            def count(i):
                for b in range(RING):
                    pe.wait_ge(s_hot, i * RING + b + 1)
                    for a in range(2):
                        last = nc.tensor.matmul(pH[0:T, a * LO:(a + 1) * LO], hot_hi[:, b, a * T:(a + 1) * T],
                                                hot_lo[:, b, :], start=False, stop=False)
                    last.then_inc(s_hist, 1)
            run(pe, T // RING, count)
            nc.tensor.matmul(pH[0:T, :], zeros[:, 0:T], zeros[:, :], start=False, stop=True).then_inc(s_pe, 1)
            pe.wait_ge(s_srt, 80)
            nc.tensor.transpose(pX[:, 3 * T:4 * T], rows[:, 3, :], ident[0:T, 0:T]).then_inc(s_pe, 1)

            def look_up(i, a):
                pe.wait_ge(s_hi, i + 1)
                for k in range(BODY):
                    n, b = step(i, k), k % LOOKS
                    pc, cs = look_banks[b], slice(k * P, (k + 1) * P)
                    wait(pe, s_looked, n - lag(k))
                    nc.tensor.matmul(pc[:, 0:P + 2], above[a][:, cs], step_lo[:, :], start=True, stop=False)
                    nc.tensor.matmul(pc[:, 0:P + 2], above[a][:, cs], step_hi[:, :], start=False, stop=True
                                     ).then_inc(s_look, 1)
            run_pairs(pe, look_up)
            pe.wait_ge(s_bcused, TURNS)
            nc.tensor.matmul(pS[0:T, 0:P], own[:, :], last_row[:, :], start=True, stop=True)
            nc.tensor.matmul(pS[0:T, P:2 * P], own[:, :], first_row[:, :], start=True, stop=True).then_inc(s_pe, 1)
            pe.wait_ge(S("v_ends"), 1)
            pe.wait_ge(S("g_runs"), 1)
            for a in range(2):
                last = nc.tensor.matmul(pS[:, 2 * P + a * T:2 * P + (a + 1) * T], ends[:, a, :], runs[:, a, :],
                                        start=True, stop=True)
            last.then_inc(s_pe, 1)
            pe.wait_ge(S("v_bias"), 1)
            ahead(lambda g, stg: dense_pe(pe, g, stg))
            pe.wait_ge(S("v_rowidx"), 1)
            phase_loop(pe, "edge", lambda i, k, stg: edge_pe(pe, i, k, stg),
                       lambda g, stg, i, j: dense_pe(pe, g, stg))
            for c in (1, 2, 3):
                phase_loop(pe, f"conv{c}", lambda i, k, stg: conv_pe(pe, c, i, k, stg),
                           lambda g, stg, i, j: dense_pe(pe, g, stg))


_INS = ["x", "src", "dst", "L0_gnn_W_edge", "L0_gnn_b_edge", "L0_gnn_W1", "L0_gnn_b1", "L0_gnn_W2", "L0_gnn_b2",
        "L0_gnn_eps", "L1_gnn_W1", "L1_gnn_b1", "L1_gnn_W2", "L1_gnn_b2", "L1_gnn_W3", "L1_gnn_b3"]


def kernel(**inputs):
    import numpy as _np
    import concourse.bacc as _bacc
    from concourse import mybir as _mybir
    from concourse.bass_utils import run_bass_kernel_spmd as _run

    nc = _bacc.Bacc("TRN2", target_bir_lowering=False, num_devices=1)
    arrays, args = {}, []
    for name in _INS:
        a = _np.ascontiguousarray(inputs[name])
        arrays[f"in_{name}"] = a
        args.append(nc.dram_tensor(f"in_{name}", a.shape, _mybir.dt.from_np(a.dtype), kind="ExternalInput").ap())
    args.append(nc.dram_tensor("out", (N, D), _mybir.dt.float32, kind="ExternalOutput").ap())
    build(nc, *args)
    r = _run(nc, [arrays], core_ids=[0])
    return r.results[0]["out"]
```

```python
import concourse.bass as bass
from concourse import mybir
from contextlib import ExitStack

N = 50000
E = 12500
D = 128
P = 128
T = -(-E // P)
EP = T * P
BODY = 14
TURNS = T // BODY
CH = BODY * P
FULL = E // P
HI, LO = 2 * T, 256
SRC_PAD = HI * LO - 1
DST_PAD, DST_END = 65535, 70000
G = 512
R = G // P
SPREAD = {"edge": 5, "conv1": 4, "conv2": 4}
LOOPED = TURNS * sum(SPREAD.values())
AHEAD = N // G - LOOPED
TAIL = N - (N // G) * G
TP = TAIL // 3
RING = 7
SLOTS = 5
STORES = 4
LOOKS = 4
LAG = 11
COUNTED = 4
EPS = 1e-5

STAGES = {"load": 0, "T": 3, "T_out": 4, "H": 5, "H_out": 6, "O": 7, "add": 8, "stats1": 9, "var1": 9,
          "sd1": 10, "rsd1": 11, "y": 11, "stats2": 12, "var2": 12, "sd2": 13, "rsd2": 14, "shift": 14,
          "norm": 15, "store": 15}
EDGE = {"T": 0, "T_out": 0, "M": 1, "M_out": 1, "N": 2, "N_out": 2, "H": 3, "H_out": 3, "O": 4,
        "add": 4, "stats": 5, "var": 5, "sd": 6, "rsd": 7, "shift": 7, "norm": 8, "store": 8}
CONV = {"scale": 0, "A": 1, "A_out": 2, "B": 3, "relu": 4, "store": 4}
CONV3 = {"A": 1, "A_out": 2, "B": 3, "add": 4, "stats": 5, "var": 5, "sd": 6, "rsd": 7, "shift": 7, "norm": 8}
SECOND = {"var", "shift", "var1", "y", "var2", "norm"}
DRAIN = {"edge": 10, "conv1": 6, "conv2": 6, "conv3": 8}
AHEAD_STEPS = 14


def build(nc, x, src, dst, W_edge, b_edge, W1, b1, W2, b2, eps, C1, c1, C2, c2, C3, c3, out):
    f32, bf16, i32 = mybir.dt.float32, mybir.dt.bfloat16, mybir.dt.int32
    ALU, ACT, AX = mybir.AluOpType, mybir.ActivationFunctionType, mybir.AxisListType
    ds = bass.ds
    ctx = ExitStack()
    with ctx:
        ctx.enter_context(nc.allow_non_contiguous_dma(reason="columns of biases and of edge ids, once"))

        def sb(name, shape, dt=f32):
            return ctx.enter_context(nc.sbuf_tensor(name, shape, dt))

        def sem(name):
            return ctx.enter_context(nc.semaphore(name))

        count_dram = nc.dram_tensor("count_dram", [HI * LO, 1], f32, kind="Internal").ap()
        ids_dram = nc.dram_tensor("ids_dram", [2, EP + 2], f32, kind="Internal").ap()
        y_dram = nc.dram_tensor("y_dram", [EP * 2, D], f32, kind="Internal").ap()
        u_dram = [nc.dram_tensor(f"u{n}_dram", [EP + 1, D], f32, kind="Internal").ap() for n in (1, 2)]

        same = sb("same", [P, EP])
        cont = sb("cont", [P, EP], bf16)
        above_a = sb("above_a", [T, CH], bf16)
        rows_i = sb("rows_i", [T, 2, P], i32)
        rows = sb("rows", [T, 4, P])
        tmp_i = sb("tmp_i", [T, P], i32)
        cols = sb("cols", [P, 5, T])
        srt = sb("srt", [T, 2, P + 2])
        srt_i = sb("srt_i", [T, P + 2], i32)
        before = sb("before", [T, 1])
        step_lo = sb("step_lo", [T, P + 2], bf16)
        step_hi = sb("step_hi", [T, P + 2], bf16)
        first_bc = sb("first_bc", [P, T])
        runs = sb("runs", [T, 2, T])
        next_bc = sb("next_bc", [P, T])
        own = sb("own", [P, T])
        ends = sb("ends", [T, 2, P])
        deg = sb("deg", [P, T])
        scale = sb("scale", [P, T])
        deg_after = sb("deg_after", [P, T])
        deg_out = sb("deg_out", [P, T])
        below = sb("below", [P, T])
        equal = sb("equal", [P, T])
        hit = sb("hit", [P, T])
        found = sb("found", [P, T])
        found_i = sb("found_i", [P, 2, T], i32)
        reach = sb("reach", [P, T])
        fidx = sb("fidx", [P, 2, T])
        idx = sb("idx", [P, 5, T], i32)
        SRC_I, DST_I, Y_I, U_I, O_I = range(5)
        stage = sb("stage", [P, 3, BODY], i32)
        ostage = sb("ostage", [P, BODY], i32)
        enum_i = sb("enum_i", [P, T], i32)
        enum = sb("enum", [P, T])
        ramp_i = sb("ramp_i", [P, LO], i32)
        ramp = sb("ramp", [P, LO], bf16)
        part_i = sb("part_i", [P, 1], i32)
        part = sb("part", [P, 3])
        ident = sb("ident", [P, P])
        last_row = sb("last_row", [P, P])
        first_row = sb("first_row", [P, P])
        hot_hi = sb("hot_hi", [P, RING, HI], bf16)
        hot_lo = sb("hot_lo", [P, RING, LO], bf16)
        tab = sb("tab", [T, 2 * LO])
        zeros = sb("zeros", [P, 512], bf16)
        mark = sb("mark", [P, 1])
        ones96 = sb("ones96", [96, P], bf16)
        braw = sb("braw", [96, 5, D])
        bhalf = sb("bhalf", [96, 5, D], bf16)
        bsplit = sb("bsplit", [96, 8, D], bf16)
        W1e = sb("W1e", [D, D])
        Wa, Wb, W1s, W2s = sb("Wa", [D, D]), sb("Wb", [D, D]), sb("W1s", [D, D]), sb("W2s", [D, D])
        Cs = [sb(f"C{n}s", [D, D]) for n in (1, 2, 3)]
        b1c = sb("b1c", [D, 1])
        eps1 = sb("eps1", [P, 1])
        epsc = sb("epsc", [P, 1])
        cb = sb("cb", [P, 3, D])
        relu_cb = sb("relu_cb", [P, 3, D])
        gx = sb("gx", [P, BODY, 2, D])
        gz = sb("gz", [P, BODY, D])
        yd = sb("yd", [P, BODY, D])
        deg_in_flight = sb("deg_in_flight", [P, BODY])
        xT = sb("xT", [P, RING, 2 * P])
        msg = sb("msg", [P, 2, D])
        aggT = sb("aggT", [P, 2, P])
        found_at = sb("found_at", [P, LOOKS, P + 2], bf16)
        dst_b = sb("dst_b", [P, CH])
        hT = sb("hT", [P, 2, 2 * P])
        res = sb("res", [P, RING, 2, D])
        st = sb("st", [P, RING, 2, 6])
        mv = sb("mv", [P, RING, 2, 2])
        sd = sb("sd", [P, RING, 2])
        rs = sb("rs", [P, RING, 2])
        shift = sb("shift", [P, RING, 2])
        yo = sb("yo", [P, STORES, 2, D])
        uo = sb("uo", [P, STORES, D])
        xin = sb("xin", [P, SLOTS, R * D])
        zout = sb("zout", [P, SLOTS, R * D])
        dst_bc = [yd[:, :, :].rearrange("p k f -> p (k f)"), dst_b[:, :]]
        src_bc = [gz[:, :, :].rearrange("p k f -> p (k f)")[0:T, :], xT[:, :, :].rearrange("p k f -> p (k f)")[0:T, :]]
        looked = [found_at[:, b, 0:P + 1] for b in range(LOOKS)]
        above = [above_a[:, :], hot_lo[:, :, :].rearrange("p b l -> p (b l)")[0:T, :]]
        drT = sb("drT", [P, G])
        dhT = sb("dhT", [P, G])
        dst1 = sb("dst1", [P, SLOTS, R, 6])
        dshift = sb("dshift", [P, SLOTS, R])
        dmv = sb("dmv", [P, SLOTS, R, 2])
        dsd = sb("dsd", [P, SLOTS, R])
        drs = sb("drs", [P, SLOTS, R])
        dst2 = sb("dst2", [P, SLOTS, R, 6])
        dmv2 = sb("dmv2", [P, SLOTS, R, 2])
        dsd2 = sb("dsd2", [P, SLOTS, R])
        drs2 = sb("drs2", [P, SLOTS, R])

        bank = [ctx.enter_context(nc.psum_tensor(f"bank{n}", [P, 512], f32)) for n in range(8)]
        pX, pM, pS, pH, pO, dX, dH, dO = bank
        look_banks = (pO, pM, dX, dH)

        s_w = sem("s_w")
        s_rows = sem("s_rows")
        s_iota = sem("s_iota")
        s_padded = sem("s_padded")
        s_v = sem("s_v")
        s_ids = sem("s_ids")
        s_pad = sem("s_pad")
        s_srt = sem("s_srt")
        s_pe = sem("s_pe")
        s_hot = sem("s_hot")
        s_hist = sem("s_hist")
        s_bc = [sem(f"s_bc_{a}") for a in range(2)]
        s_bcused = sem("s_bcused")
        s_hi = sem("s_hi")
        s_table = sem("s_table")
        s_look = sem("s_look")
        s_looked = sem("s_looked")
        s_root = sem("s_root")
        s_ci = sem("s_ci")
        s_const_u = sem("s_const_u")
        s_held = sem("s_held")
        PHASES = ["edge", "conv1", "conv2", "conv3"]
        HALF = BODY // 2
        gat = [sem(f"gat_{k}") for k in range(BODY)]
        stored = [sem(f"stored_{k}") for k in range(STORES)]
        yd_in = [sem(f"yd_in_{h}") for h in range(2)]
        s_counts = [sem(f"s_counts_{h}") for h in range(2)]
        d_in = [sem(f"d_in_{k}") for k in range(SLOTS)]
        d_out = [sem(f"d_out_{k}") for k in range(SLOTS)]
        ev = {}

        def S(name):
            if name not in ev:
                ev[name] = sem(name)
            return ev[name]

        def wait(eng, semaphore, value):
            if not isinstance(value, int) or value > 0:
                eng.wait_ge(semaphore, value)

        def take_waits(eng):
            eng.sem_inc(s_held, 1)

        def step(i, k):
            return i * BODY + k

        def gathered(phase, i):
            if phase == "edge":
                return i * 32 + 32
            before = TURNS * (32 + 16 * (int(phase[4]) - 1))
            return i * 32 + (before + 16) if phase == "conv3" else i * 16 + (before + 16)

        def turns(k, slots=BODY):
            return len(range(k, BODY, slots))

        def stored_before(phase, i, k):
            slot = k % STORES
            return i * (16 * turns(slot, STORES)) + 16 * (k // STORES + PHASES.index(phase) * TURNS * turns(slot, STORES))

        def all_stored(eng, phase):
            for slot in range(STORES):
                eng.wait_ge(stored[slot], 16 * turns(slot, STORES) * TURNS * (PHASES.index(phase) + 1))

        def half_sem(name, k):
            return S(f"{name}_{k // HALF}")

        def wait_tile(eng, name, i, k):
            if k < 0:
                wait(eng, half_sem(name, BODY + k), i * HALF + (k + 1))
            else:
                wait(eng, half_sem(name, k), i * HALF + (k % HALF + 1))

        class Group:
            def __init__(self, n, slot, uses, rows_, parts, start, phase="ahead"):
                self.n, self.slot, self.uses, self.r, self.p, self.start = n, slot, uses, rows_, parts, start
                self.in_bank = phase in ("conv1", "conv2")
                self.out = (dO, pO)[slot % 2] if self.in_bank else dO

            def dram(self, a):
                return a[ds(self.start, self.r * self.p), :].rearrange("(p k) d -> p (k d)", k=self.r)

        def ahead_group(m):
            slot = (m - (AHEAD + 1)) % SLOTS
            if m == AHEAD:
                return Group(m, slot, m // SLOTS, 3, TP, (N // G) * G)
            return Group(m, slot, m // SLOTS, R, P, m * G)

        def ahead_in_slot(j):
            return sum(ahead_group(m).slot == j for m in range(AHEAD + 1))

        def turns_of_slot(phases, j):
            return TURNS * sum(j < SPREAD[q] for q in phases)

        def looped_group(phase, i, j):
            earlier = PHASES[:PHASES.index(phase)]
            groups = TURNS * sum(SPREAD[q] for q in earlier)
            uses = ahead_in_slot(j) + turns_of_slot(earlier, j)
            return Group(i * SPREAD[phase] + (groups + AHEAD + 1 + j), j, i + uses, R, P,
                         i * (SPREAD[phase] * G) + (AHEAD + groups + j) * G, phase)

        def dense_pe(pe, g, stg):
            w, r = g.p, g.r
            if stg == "T":
                pe.wait_ge(d_in[g.slot], g.uses * 16 + 16)
                wait(pe, S("d_xT_out"), g.n)
                for k in range(r):
                    last = nc.tensor.transpose(dX[:, k * w:(k + 1) * w], xin[0:w, g.slot, k * D:(k + 1) * D],
                                               ident[0:w, 0:w])
                last.then_inc(S("d_xT"), 1)
            if stg == "H":
                pe.wait_ge(S("d_xT_out"), g.n + 1)
                wait(pe, S("d_h_out"), g.n)
                nc.tensor.matmul(dH[:, 0:r * w], W1s[:, :], drT[:, 0:r * w], start=True, stop=True
                                 ).then_inc(S("d_h"), 1)
            if stg == "O":
                pe.wait_ge(S("d_h_out"), g.n + 1)
                if g.in_bank:
                    pe.wait_ge(S("d_y"), g.n - 1)
                else:
                    wait(pe, S("d_o_out"), g.n)
                nc.tensor.matmul(g.out[0:w, 0:r * D], ones96[:, 0:w], bsplit[:, 1:1 + r, :].rearrange("p a d -> p (a d)"),
                                 start=True, stop=False)
                for k in range(r):
                    last = nc.tensor.matmul(g.out[0:w, k * D:(k + 1) * D], dhT[:, k * w:(k + 1) * w], W2s[:, :],
                                            start=False, stop=(k == r - 1 and not g.in_bank))
                if g.in_bank:
                    last = nc.tensor.matmul(g.out[0:w, 0:r * D], ident[:, :], xin[0:w, g.slot, 0:r * D],
                                            start=False, stop=True)
                last.then_inc(S("d_o"), 1)

        def dense_act(act, g, stg):
            w, r = g.p, g.r
            if stg == "T_out":
                act.wait_ge(S("d_xT"), g.n + 1)
                wait(act, S("d_h"), g.n)
                nc.scalar.activation(drT[:, 0:r * w], dX[:, 0:r * w], ACT.Identity, scale=eps1[:, 0:1]
                                     ).then_inc(S("d_xT_out"), 1)
            if stg == "H_out":
                act.wait_ge(S("d_h"), g.n + 1)
                wait(act, S("d_o"), g.n)
                nc.scalar.activation(dhT[:, 0:r * w], dH[:, 0:r * w], ACT.Relu, bias=b1c[:, 0:1]
                                     ).then_inc(S("d_h_out"), 1)
            s = g.slot
            if stg == "sd1":
                act.wait_ge(S("d_var1"), g.n + 1)
                nc.scalar.activation(dsd[0:w, s, 0:r], dmv[0:w, s, 0:r, 1], ACT.Sqrt, bias=epsc[0:w, 0:1]
                                     ).then_inc(S("d_sd1"), 1)
            if stg == "sd2":
                act.wait_ge(S("d_var2"), g.n + 1)
                nc.scalar.activation(dsd2[0:w, s, 0:r], dmv2[0:w, s, 0:r, 1], ACT.Sqrt, bias=epsc[0:w, 0:1]
                                     ).then_inc(S("d_sd2"), 1)
            if stg == "norm":
                act.wait_ge(S("d_shift"), g.n + 1)
                for k in range(r):
                    row = zout[0:w, s, k * D:(k + 1) * D]
                    last = nc.scalar.activation(row, row, ACT.Identity, scale=drs2[0:w, s, k:k + 1],
                                                bias=dshift[0:w, s, k:k + 1])
                last.then_inc(S("d_z"), 1)

        def dense_dve(dve, g, stg):
            w, r, s = g.p, g.r, g.slot
            total = g.out[0:w, 0:r * D] if g.in_bank else xin[0:w, s, 0:r * D]
            if stg == "add" and not g.in_bank:
                dve.wait_ge(S("d_o"), g.n + 1)
                nc.vector.tensor_tensor(total, dO[0:w, 0:r * D], xin[0:w, s, 0:r * D], ALU.add
                                        ).then_inc(S("d_o_out"), 1)
            if stg == "stats1":
                if g.in_bank:
                    dve.wait_ge(S("d_o"), g.n + 1)
                else:
                    dve.wait_ge(S("d_o_out"), g.n + 1)
                for k in range(r):
                    last = nc.vector.bn_stats(dst1[0:w, s, k, :], total[:, k * D:(k + 1) * D])
                last.then_inc(S("d_st1"), 1)
            if stg == "var1":
                dve.wait_ge(S("d_st1"), g.n + 1)
                take_waits(dve)
                for k in range(r):
                    last = nc.vector.bn_aggr(dmv[0:w, s, k, :], dst1[0:w, s, k, :])
                last.then_inc(S("d_var1"), 1)
            if stg == "rsd1":
                dve.wait_ge(S("d_sd1"), g.n + 1)
                nc.vector.reciprocal(drs[0:w, s, 0:r], dsd[0:w, s, 0:r]).then_inc(S("d_rs1"), 1)
            if stg == "y":
                dve.wait_ge(S("d_rs1"), g.n + 1)
                wait(dve, d_out[s], g.uses * 16)
                for k in range(r):
                    last = nc.vector.scalar_tensor_tensor(zout[0:w, s, k * D:(k + 1) * D],
                                                          total[:, k * D:(k + 1) * D], drs[0:w, s, k:k + 1],
                                                          relu_cb[0:w, 2, :], ALU.mult, ALU.add)
                last.then_inc(S("d_y"), 1)
            if stg == "stats2":
                dve.wait_ge(S("d_y"), g.n + 1)
                for k in range(r):
                    last = nc.vector.bn_stats(dst2[0:w, s, k, :], zout[0:w, s, k * D:(k + 1) * D])
                last.then_inc(S("d_st2"), 1)
            if stg == "var2":
                dve.wait_ge(S("d_st2"), g.n + 1)
                take_waits(dve)
                for k in range(r):
                    last = nc.vector.bn_aggr(dmv2[0:w, s, k, :], dst2[0:w, s, k, :])
                last.then_inc(S("d_var2"), 1)
            if stg == "rsd2":
                dve.wait_ge(S("d_sd2"), g.n + 1)
                nc.vector.reciprocal(drs2[0:w, s, 0:r], dsd2[0:w, s, 0:r]).then_inc(S("d_rs2"), 1)
            if stg == "shift":
                dve.wait_ge(S("d_rs2"), g.n + 1)
                nc.vector.scalar_tensor_tensor(dshift[0:w, s, 0:r], dmv2[0:w, s, 0:r, 0], -1.0, drs2[0:w, s, 0:r],
                                               ALU.mult, ALU.mult).then_inc(S("d_shift"), 1)

        def dense_sp(sp, g, stg, free):
            if stg == "load":
                wait(sp, S("d_y"), free)
                sp.dma_start(xin[0:g.p, g.slot, 0:g.r * D], g.dram(x)).then_inc(d_in[g.slot], 16)
            if stg == "store":
                sp.wait_ge(S("d_z"), g.n + 1)
                sp.dma_start(g.dram(out), zout[0:g.p, g.slot, 0:g.r * D]).then_inc(d_out[g.slot], 16)

        def edge_pe(pe, i, k, stg):
            n, b, c = step(i, k), k % 2, k % RING
            if stg == "T":
                pe.wait_ge(gat[k], gathered("edge", i))
                wait(pe, S("e_x_out"), n)
                nc.tensor.transpose(pX[:, 0:P], gx[:, k, 0, :], ident[:, :])
                nc.tensor.transpose(pX[:, P:2 * P], gx[:, k, 1, :], ident[:, :]).then_inc(S("e_x"), 1)
            if stg == "M":
                pe.wait_ge(S("e_x_out"), n + 1)
                wait(pe, S("e_m_out"), n)
                nc.tensor.matmul(pM[:, 0:D], ones96[:, :], bsplit[:, 0, :], start=True, stop=False)
                nc.tensor.matmul(pM[:, 0:D], xT[:, c, 0:P], Wa[:, :], start=False, stop=False)
                nc.tensor.matmul(pM[:, 0:D], xT[:, c, P:2 * P], Wb[:, :], start=False, stop=True
                                 ).then_inc(S("e_m"), 1)
            if stg == "N":
                pe.wait_ge(S("e_m_out"), n + 1)
                wait(pe, S("e_n_out"), n)
                nc.tensor.matmul(pS[:, 0:P], msg[:, b, :], same[:, ds(n * P, P)], start=True, stop=True
                                 ).then_inc(S("e_n"), 1)
            if stg == "H":
                pe.wait_ge(S("e_n_out"), n + 1)
                wait(pe, S("e_h_out"), n)
                nc.tensor.matmul(pH[:, 0:2 * P], W1e[:, :], xT[:, c, :], start=True, stop=False)
                nc.tensor.matmul(pH[:, P:2 * P], W1s[:, :], aggT[:, b, :], start=False, stop=True
                                 ).then_inc(S("e_h"), 1)
            if stg == "O":
                pe.wait_ge(S("e_h_out"), n + 1)
                wait_tile(pe, "e_o_out", i, k - 1)
                nc.tensor.matmul(pO[:, 0:2 * D], ones96[:, :], bsplit[:, 1:3, :].rearrange("p a d -> p (a d)"),
                                 start=True, stop=False)
                for a in range(2):
                    last = nc.tensor.matmul(pO[:, a * D:(a + 1) * D], hT[:, b, a * P:(a + 1) * P], W2s[:, :],
                                            start=False, stop=(a == 1))
                last.then_inc(S("e_o"), 1)

        def edge_act(act, i, k, stg):
            n, b, c = step(i, k), k % 2, k % RING
            if stg == "T_out":
                act.wait_ge(S("e_x"), n + 1)
                wait(act, S("e_h"), n - (RING - 1))
                nc.scalar.copy(xT[:, c, :], pX[:, 0:2 * P]).then_inc(S("e_x_out"), 1)
            if stg == "M_out":
                act.wait_ge(S("e_m"), n + 1)
                wait(act, S("e_n"), n - 1)
                nc.scalar.activation(msg[:, b, :], pM[:, 0:D], ACT.Relu).then_inc(S("e_m_out"), 1)
            if stg == "H_out":
                act.wait_ge(S("e_h"), n + 1)
                wait(act, S("e_o"), n - 1)
                nc.scalar.activation(hT[:, b, :], pH[:, 0:2 * P], ACT.Relu, bias=b1c[:, 0:1]).then_inc(S("e_h_out"), 1)
            if stg == "sd":
                act.wait_ge(S("e_var"), n + 1)
                nc.scalar.activation(sd[:, c, :], mv[:, c, :, 1], ACT.Sqrt, bias=epsc[:, 0:1]).then_inc(S("e_sd"), 1)
            if stg == "norm":
                slot = k % STORES
                act.wait_ge(S("e_shift"), n + 1)
                wait(act, stored[slot], stored_before("edge", i, k))
                for a in range(2):
                    last = nc.scalar.activation(yo[:, slot, a, :], res[:, c, a, :], ACT.Identity,
                                                scale=rs[:, c, a:a + 1], bias=shift[:, c, a:a + 1])
                last.then_inc(S("e_y"), 1)

        def edge_dve(dve, i, k, stg):
            n, b, c = step(i, k), k % 2, k % RING
            if stg == "N_out":
                dve.wait_ge(S("e_n"), n + 1)
                wait(dve, S("e_n_out"), n)
                wait(dve, S("e_h"), n - 1)
                nc.vector.scalar_tensor_tensor(aggT[:, b, :], cont[:, ds(n * P, P)], aggT[:, 1 - b, P - 1:P],
                                               pS[:, 0:P], ALU.mult, ALU.add).then_inc(S("e_n_out"), 1)
            if stg == "add":
                dve.wait_ge(S("e_o"), n + 1)
                wait(dve, S("e_y"), n - (RING - 1))
                nc.vector.tensor_tensor(res[:, c, :, :].rearrange("p a d -> p (a d)"), pO[:, 0:2 * D],
                                        gx[:, k, :, :].rearrange("p a d -> p (a d)"), ALU.add
                                        ).then_inc(half_sem("e_o_out", k), 1)
            if stg == "stats":
                wait_tile(dve, "e_o_out", i, k)
                for a in range(2):
                    last = nc.vector.bn_stats(st[:, c, a, :], res[:, c, a, :])
                last.then_inc(S("e_st"), 1)
            if stg == "var":
                dve.wait_ge(S("e_st"), n + 1)
                take_waits(dve)
                for a in range(2):
                    last = nc.vector.bn_aggr(mv[:, c, a, :], st[:, c, a, :])
                last.then_inc(S("e_var"), 1)
            if stg == "rsd":
                dve.wait_ge(S("e_sd"), n + 1)
                nc.vector.reciprocal(rs[:, c, :], sd[:, c, :]).then_inc(S("e_rs"), 1)
            if stg == "shift":
                dve.wait_ge(S("e_rs"), n + 1)
                nc.vector.scalar_tensor_tensor(shift[:, c, :], mv[:, c, :, 0], -1.0, rs[:, c, :], ALU.mult, ALU.mult
                                               ).then_inc(S("e_shift"), 1)

        def edge_sp(sp, i, k, stg):
            n = step(i, k)
            if stg == "store":
                sp.wait_ge(S("e_y"), n + 1)
                sp.dma_start(y_dram[ds(n * (2 * P), 2 * P), :].rearrange("(p a) d -> p (a d)", a=2),
                             yo[:, k % STORES, :, :].rearrange("p a d -> p (a d)")
                             ).then_inc(stored[k % STORES], 16)

        def conv_pe(pe, c, i, k, stg):
            q, n, b = f"conv{c}", step(i, k), k % 2
            m = n + (c - 1) * T
            if stg == "A":
                pe.wait_ge(gat[k], gathered(q, i))
                if c == 1:
                    pe.wait_ge(S("c1_scaled"), n + 1)
                wait(pe, S("c_a_out"), m - 1)
                nc.tensor.matmul((pX, pS)[b][:, 0:P], gx[:, k, 0, :], same[:, ds(n * P, P)], start=True, stop=True
                                 ).then_inc(half_sem("c_a", k), 1)
            if stg == "B":
                pe.wait_ge(S("c_a_out"), m + 1)
                if c < 3:
                    wait(pe, S("c_u"), m - 1)
                else:
                    pe.wait_ge(S("c_u"), 2 * T)
                    wait_tile(pe, "c3_r", i, k - 2)
                nc.tensor.matmul((pM, pH)[b][:, 0:D], ones96[:, :], bsplit[:, 4 + c, :], start=True, stop=False)
                nc.tensor.matmul((pM, pH)[b][:, 0:D], aggT[:, b, :], Cs[c - 1][:, :], start=False, stop=True
                                 ).then_inc(S("c_b"), 1)

        def conv_dve(dve, c, i, k, stg):
            n, b = step(i, k), k % 2
            m = n + (c - 1) * T
            if stg == "A_out":
                wait_tile(dve, "c_a", i + (c - 1) * TURNS, k)
                wait(dve, S("c_b"), m - 1)
                wait(dve, S("c_a_out"), m)
                nc.vector.scalar_tensor_tensor(aggT[:, b, :], cont[:, ds(n * P, P)], aggT[:, 1 - b, P - 1:P],
                                               (pX, pS)[b][:, 0:P], ALU.mult, ALU.add).then_inc(S("c_a_out"), 1)
            if c == 3:
                r = k % RING
                if stg == "add":
                    dve.wait_ge(S("c_b"), m + 1)
                    dve.wait_ge(yd_in[k // HALF], i * (16 * HALF) + 16 * HALF)
                    wait(dve, S("c3_z"), n - (RING - 1))
                    nc.vector.scalar_tensor_tensor(res[:, r, 0, :], (pM, pH)[b][:, 0:D], 0.0, yd[:, k, :], ALU.max, ALU.add
                                                   ).then_inc(half_sem("c3_r", k), 1)
                if stg == "stats":
                    wait_tile(dve, "c3_r", i, k)
                    nc.vector.bn_stats(st[:, r, 0, :], res[:, r, 0, :]).then_inc(S("c3_st"), 1)
                if stg == "var":
                    dve.wait_ge(S("c3_st"), n + 1)
                    take_waits(dve)
                    nc.vector.bn_aggr(mv[:, r, 0, :], st[:, r, 0, :]).then_inc(S("c3_var"), 1)
                if stg == "rsd":
                    dve.wait_ge(S("c3_sd"), n + 1)
                    nc.vector.reciprocal(rs[:, r, 0:1], sd[:, r, 0:1]).then_inc(S("c3_rs"), 1)
                if stg == "shift":
                    dve.wait_ge(S("c3_rs"), n + 1)
                    nc.vector.scalar_tensor_tensor(shift[:, r, 0:1], mv[:, r, 0, 0:1], -1.0, rs[:, r, 0:1],
                                                   ALU.mult, ALU.mult).then_inc(S("c3_shift"), 1)

        def conv_act(act, c, i, k, stg):
            n, b = step(i, k), k % 2
            m = n + (c - 1) * T
            if stg == "scale" and c == 1:
                nc.scalar.activation(same[:, ds(n * P, P)], same[:, ds(n * P, P)], ACT.Identity,
                                     scale=scale[:, ds(n, 1)]).then_inc(S("c1_scaled"), 1)
            if stg == "relu" and c < 3:
                slot = k % STORES
                act.wait_ge(S("c_b"), m + 1)
                act.wait_ge(stored[slot], stored_before(f"conv{c}", i, k))
                nc.scalar.activation(uo[:, slot, :], (pM, pH)[b][:, 0:D], ACT.Relu).then_inc(S("c_u"), 1)
            if c == 3:
                r = k % RING
                if stg == "sd":
                    act.wait_ge(S("c3_var"), n + 1)
                    nc.scalar.activation(sd[:, r, 0:1], mv[:, r, 0, 1:2], ACT.Sqrt, bias=epsc[:, 0:1]
                                         ).then_inc(S("c3_sd"), 1)
                if stg == "norm":
                    act.wait_ge(S("c3_shift"), n + 1)
                    nc.scalar.activation(gz[:, k, :], res[:, r, 0, :], ACT.Identity, scale=rs[:, r, 0:1],
                                         bias=shift[:, r, 0:1]).then_inc(S("c3_z"), 1)

        def conv_sp(sp, c, i, k, stg):
            n = step(i, k)
            m = n + (c - 1) * T
            if stg == "store" and c < 3:
                sp.wait_ge(S("c_u"), m + 1)
                sp.dma_start(u_dram[c - 1][ds(n * P, P), :], uo[:, k % STORES, :]
                             ).then_inc(stored[k % STORES], 16)

        def run(eng, count, turn):
            turn(0)
            with eng.Fori(1, count) as i:
                turn(i)

        def run_pairs(eng, turn):
            turn(0, 0)
            with eng.Fori(1, (TURNS + 1) // 2) as i:
                turn(i * 2 - 1, 1)
                turn(i * 2, 0)

        def lag(k):
            return (LOOKS if k >= LOOKS else k + BODY - max(q for q in range(BODY) if q % LOOKS == k)) - 1

        def ahead_stages(t):
            return [(ahead_group(m), stg) for m in range(AHEAD + 1) for stg, off in STAGES.items() if 2 * m + off == t]

        def looped_stages(phase, i, t, second=None):
            return [(looped_group(phase, i, j), stg) for j in reversed(range(SPREAD.get(phase, 0)))
                    for stg, off in sorted(STAGES.items(), key=lambda kv: -kv[1])
                    if j * BODY // SPREAD[phase] + off == t and second in (None, stg in SECOND)]

        def carried_stages(before, t):
            if before == "ahead":
                return ahead_stages(AHEAD_STEPS + t)
            if before is None:
                return []
            return looped_stages(before, TURNS - 1, BODY + DRAIN[before] + t)

        def free_after(phase, i, j):
            n = looped_group(phase, i, j).n
            if isinstance(i, int) and i == 0:
                before = PHASES[PHASES.index(phase) - 1]
                return n + 1 - (SLOTS if phase == "edge" else SPREAD[before])
            return n + 1 - SPREAD[phase]

        def phase_loop(eng, phase, before, tile_fn, dense_fn, last=lambda: None):
            stages = {"edge": EDGE, "conv1": CONV, "conv2": CONV, "conv3": CONV3}[phase]
            late_first = sorted(stages.items(), key=lambda kv: -kv[1])

            def steps(i, has_tiles, has_before, count=BODY):
                for t in range(count):
                    for second in (False, True):
                        for stg, off in late_first:
                            if (stg in SECOND) == second:
                                if t >= off and has_tiles:
                                    tile_fn(i, t - off, stg)
                                if t < off and has_before:
                                    tile_fn(i - 1, t - off + BODY, stg)
                        if has_tiles:
                            for g, stg in looped_stages(phase, i, t, second):
                                dense_fn(g, stg, free_after(phase, i, g.slot))
                        if has_before:
                            for g, stg in looped_stages(phase, i - 1, t + BODY, second):
                                dense_fn(g, stg, None)
                        if has_tiles and not has_before:
                            for g, stg in carried_stages(before, t):
                                if (stg in SECOND) == second:
                                    dense_fn(g, stg, None)

            steps(0, True, False)
            with eng.Fori(1, TURNS) as i:
                steps(i, True, True)
            last()
            steps(TURNS, False, True, DRAIN[phase])

        def ahead(dense_fn):
            for t in range(AHEAD_STEPS):
                for g, stg in ahead_stages(t):
                    dense_fn(g, stg, g.n - SLOTS + 1)

        block = ctx.enter_context(nc.Block())

        @block.sync
        def _(sp):
            sp.wait_ge(s_pad, 1)
            for a, v in ((0, src), (1, dst)):
                sp.dma_start(rows_i[0:FULL, a, :], v[0:FULL * P].rearrange("(t p) -> t p", p=P)).then_inc(s_rows, 16)
                sp.dma_start(rows_i[FULL:FULL + 1, a, 0:E - FULL * P],
                             v[FULL * P:E].rearrange("(t p) -> t p", t=1)).then_inc(s_rows, 16)
            for tile_, w in ((Wa, W_edge[0:D, :]), (Wb, W_edge[D:2 * D, :]), (W1s, W1), (W2s, W2),
                             (Cs[0], C1), (Cs[1], C2), (Cs[2], C3)):
                sp.dma_start(tile_[:, :], w).then_inc(s_w, 16)
            sp.dma_start(b1c[:, :], b1.rearrange("(p a) -> p a", a=1)).then_inc(s_w, 16)
            sp.dma_start(eps1[:, :], eps.rearrange("(p a) -> p a", a=1).to_broadcast([P, 1])).then_inc(s_w, 16)
            for a, v in enumerate((c1, c2, c3)):
                sp.dma_start(cb[:, a, :], v.rearrange("(a d) -> a d", a=1).to_broadcast([P, D])).then_inc(s_w, 16)
            for a, v in enumerate((b_edge, b2, c1, c2, c3)):
                sp.dma_start(braw[:, a, :], v.rearrange("(a d) -> a d", a=1).to_broadcast([96, D])).then_inc(s_w, 16)
            sp.wait_ge(s_padded, 1)
            for a in range(2):
                sp.dma_start(ids_dram[a, 1:1 + EP].rearrange("(t p) -> t p", p=P), rows[:, a, :]).then_inc(s_ids, 16)
            sp.dma_start(ids_dram[1:2, 0:1], part[0:1, 0:1]).then_inc(s_ids, 16)
            sp.dma_start(ids_dram[1:2, EP + 1:EP + 2], part[0:1, 2:3]).then_inc(s_ids, 16)
            sp.wait_ge(s_ids, 16 * 4)
            sp.dma_start(rows[:, 3, :], ids_dram[1, 2:2 + EP].rearrange("(t p) -> t p", p=P)).then_inc(s_srt, 16)
            sp.dma_start(srt[:, 0, 0:1], ids_dram[1, 0:EP].rearrange("(t p) -> t p", p=P)[:, 0:1]).then_inc(s_srt, 16)
            sp.dma_start(srt[:, 0, 1:1 + P], ids_dram[1, 1:1 + EP].rearrange("(t p) -> t p", p=P)).then_inc(s_srt, 16)
            sp.dma_start(srt[1:T, 1, 0:1], ids_dram[1, 0:EP - P].rearrange("(t p) -> t p", p=P)[:, 0:1]).then_inc(s_srt, 16)
            sp.dma_start(srt[1:T, 1, 1:1 + P], ids_dram[1, 1:1 + EP - P].rearrange("(t p) -> t p", p=P)).then_inc(s_srt, 16)
            def spread_ids(i, a):
                wait(sp, s_bcused, i - 1)
                for v, ids_bc, w in ((0, src_bc[a], T), (1, dst_bc[a], P)):
                    sp.dma_start(ids_bc, ids_dram[v:v + 1, ds(i * CH + 1, CH)].to_broadcast([w, CH])
                                 ).then_inc(s_bc[a], 16)
            spread_ids(0, 0)
            sp.wait_ge(s_ci, 1)
            for a in range(2):
                sp.dma_start(u_dram[a][EP:EP + 1, :], relu_cb[0:1, a, :]).then_inc(s_const_u, 16)
            sp.wait_ge(S("v_tab"), 1)
            for a in range(2):
                sp.dma_start(count_dram[a * T * LO:(a + 1) * T * LO, :].rearrange("(p l) o -> p (l o)", l=LO),
                             tab[:, a * LO:(a + 1) * LO]).then_inc(s_table, 16)

            with sp.Fori(1, (TURNS + 1) // 2) as i:
                spread_ids(i * 2 - 1, 1)
                spread_ids(i * 2, 0)
            ahead(lambda g, stg, free: dense_sp(sp, g, stg, free))
            phase_loop(sp, "edge", "ahead", lambda i, k, stg: edge_sp(sp, i, k, stg),
                       lambda g, stg, free: dense_sp(sp, g, stg, free))
            for c in (1, 2):
                phase_loop(sp, f"conv{c}", PHASES[c - 1], lambda i, k, stg: conv_sp(sp, c, i, k, stg),
                           lambda g, stg, free: dense_sp(sp, g, stg, free))

            def load_y(i):
                for k in range(BODY):
                    n = step(i, k)
                    if k % HALF == 0:
                        wait(sp, half_sem("c3_r", k), i * HALF)
                    sp.dma_start(yd[:, k, :], y_dram[ds(n * (2 * P), 2 * P), :].rearrange(
                        "(p a) d -> p a d", a=2)[:, 1, :]).then_inc(yd_in[k // HALF], 16)
            load_y(0)
            for t in range(BODY):
                for g, stg in carried_stages("conv2", t):
                    dense_sp(sp, g, stg, None)
            with sp.Fori(1, TURNS) as i:
                load_y(i)
            for k in range(BODY):
                sp.wait_ge(gat[k], gathered("conv3", TURNS - 1) + 16)

        @block.gpsimd
        def _(pool):
            nc.gpsimd.memset(rows_i[:, 0, :], SRC_PAD)
            nc.gpsimd.memset(rows_i[:, 1, :], DST_PAD).then_inc(S("g_m"), 1)
            nc.gpsimd.memset(ident[:, :], 0.0)
            nc.gpsimd.memset(first_row[:, :], 1.0)
            nc.gpsimd.memset(last_row[:, :], 1.0).then_inc(S("g_z"), 1)
            nc.gpsimd.iota(enum_i[:, :], [[P, T]], base=0, channel_multiplier=1)
            nc.gpsimd.iota(ramp_i[:, :], [[1, LO]], base=0, channel_multiplier=0)
            nc.gpsimd.iota(part_i[:, :], [[0, 1]], base=0, channel_multiplier=1).then_inc(s_iota, 1)
            pool.wait_ge(S("g_z"), 1)
            pool.wait_ge(S("g_m"), 1)
            nc.gpsimd.affine_select(out=ident[:, :], in_=ident[:, :], compare_op=ALU.not_equal, fill=1.0, base=0,
                                    pattern=[[-1, P]], channel_multiplier=1).then_inc(s_pad, 1)
            nc.gpsimd.affine_select(out=last_row[:, :], in_=last_row[:, :], compare_op=ALU.is_ge, fill=0.0,
                                    base=-(P - 1), pattern=[[0, P]], channel_multiplier=1).then_inc(s_iota, 1)
            nc.gpsimd.affine_select(out=first_row[:, :], in_=first_row[:, :], compare_op=ALU.is_ge, fill=0.0,
                                    base=0, pattern=[[0, P]], channel_multiplier=-1).then_inc(s_iota, 1)
            pool.wait_ge(S("v_runs"), 1)
            nc.gpsimd.affine_select(out=runs[:, 0, :], in_=runs[:, 0, :], compare_op=ALU.is_ge, fill=0.0, base=0,
                                    pattern=[[1, T]], channel_multiplier=-1)
            nc.gpsimd.affine_select(out=runs[:, 1, :], in_=runs[:, 1, :], compare_op=ALU.is_ge, fill=0.0, base=0,
                                    pattern=[[-1, T]], channel_multiplier=1).then_inc(S("g_runs"), 1)

            def halves(h):
                return range(h * HALF, (h + 1) * HALF)

            def take_indices(to, column, i, h, signal, count):
                take_waits(pool)
                nc.gpsimd.tensor_copy(to[:, h * HALF:(h + 1) * HALF], idx[:, column, ds(i * BODY + h * HALF, HALF)]
                                      ).then_inc(signal, 1)
                pool.wait_ge(signal, count)
                take_waits(pool)

            def gather(to, table, index):
                return nc.gpsimd.indirect_dma_start(to, None, table, bass.IndirectOffsetOnAxis(ap=index, axis=0))

            def edge_gathers(i):
                for h in range(2):
                    wait(pool, S("e_x_out"), i * BODY - BODY + (h + 1) * HALF)
                    take_indices(stage[:, 1, :], DST_I, i, h, S("g_dst"), i * 2 + h + 1)
                    take_indices(stage[:, 0, :], SRC_I, i, h, S("g_src"), i * 2 + h + 1)
                    for k in halves(h):
                        if not isinstance(i, int):
                            wait_tile(pool, "e_o_out", i - 1, k)
                            take_waits(pool)
                        gather(gx[:, k, 0, :], x, stage[:, 0, k:k + 1]).then_inc(gat[k], 16)
                        gather(gx[:, k, 1, :], x, stage[:, 1, k:k + 1]).then_inc(gat[k], 16)

            def conv_indices(c, i, h):
                wait(pool, S(f"c_a_{h}"), i * HALF + (c - 1) * (TURNS * HALF))
                take_indices(stage[:, 0, :], Y_I if c == 1 else U_I, i, h, S("g_row"), (i + (c - 1) * TURNS) * 2 + h + 1)

            def conv_gather(c, k):
                gather(gx[:, k, 0, :], (y_dram, u_dram[0], u_dram[1])[c - 1], stage[:, 0, k:k + 1]).then_inc(gat[k], 16)

            def conv_gathers(c, i, h):
                conv_indices(c, i, h)
                for k in halves(h):
                    conv_gather(c, k)

            def scatter(i, k):
                if k % HALF == 0:
                    h = k // HALF
                    for kk in halves(h):
                        pool.wait_ge(gat[kk], gathered("conv3", i))
                    take_indices(ostage, O_I, i, h, S("g_out"), i * 2 + h + 1)
                pool.wait_ge(S("c3_z"), i * BODY + (k + 1))
                take_waits(pool)
                nc.gpsimd.indirect_dma_start(
                    out, bass.IndirectOffsetOnAxis(ap=ostage[:, k:k + 1], axis=0), gz[:, k, :], None,
                    bounds_check=N - 1, oob_is_err=False).then_inc(gat[k], 16)

            pool.wait_ge(S("v_idx"), 1)
            edge_gathers(0)

            def take_counts(i, h):
                pool.wait_ge(s_counts[h], i * (16 * HALF) + 16 * HALF)
                take_waits(pool)
                nc.gpsimd.tensor_copy(deg_out[:, ds(i * BODY + h * HALF, HALF)], deg_in_flight[:, h * HALF:(h + 1) * HALF]
                                      ).then_inc(S("g_counted"), 1)

            def count_gathers(i):
                for h in range(2):
                    if not isinstance(i, int) or i > 0:
                        take_counts(i - 1, h)
                        pool.wait_ge(S("g_counted"), i * 2 + h - 1)
                    take_indices(stage[:, 2, :], SRC_I, i, h, S("g_cnt"), i * 2 + h + 1)
                    for k in halves(h):
                        gather(deg_in_flight[:, k:k + 1], count_dram, stage[:, 2, k:k + 1]).then_inc(s_counts[h], 16)
            pool.wait_ge(s_table, 32)
            run(pool, COUNTED, count_gathers)
            with pool.Fori(1, TURNS - COUNTED + 1) as i:
                edge_gathers(i)
                count_gathers(i + (COUNTED - 1))
            with pool.Fori(TURNS - COUNTED + 1, TURNS) as i:
                edge_gathers(i)
            for h in range(2):
                take_counts(TURNS - 1, h)
            all_stored(pool, "edge")
            pool.wait_ge(S("v_rowidx"), 1)
            run(pool, TURNS, lambda i: (conv_gathers(1, i, 0), conv_gathers(1, i, 1)))
            all_stored(pool, "conv1")
            pool.wait_ge(s_const_u, 32)
            run(pool, TURNS, lambda i: (conv_gathers(2, i, 0), conv_gathers(2, i, 1)))
            all_stored(pool, "conv2")
            def last_turn(i, has_tiles, has_before):
                for k in range(BODY):
                    if k == LAG and not has_before:
                        for j in range(SLOTS):
                            pool.wait_ge(d_out[j], 16 * (ahead_in_slot(j) + turns_of_slot(PHASES[:3], j)))
                    if has_tiles:
                        if k % HALF == 0:
                            conv_indices(3, i, k // HALF)
                        conv_gather(3, k)
                    if k >= LAG and has_tiles:
                        scatter(i, k - LAG)
                    if k < LAG and has_before:
                        scatter(i - 1, k - LAG + BODY)
            last_turn(0, True, False)
            with pool.Fori(1, TURNS) as i:
                last_turn(i, True, True)
            last_turn(TURNS, False, True)

        @block.vector
        def _(dve):
            count = [0]

            def link(ins):
                count[0] += 1
                ins.then_inc(s_v, 1)
                dve.wait_ge(s_v, count[0])

            V = nc.vector
            V.memset(zeros[:, :], 0.0)
            V.memset(ones96[:, :], 0.0)
            V.memset(bsplit[:, :, :], 0.0)
            V.memset(epsc[:, :], EPS)
            V.memset(aggT[:, :, :], 0.0)
            V.memset(srt[:, :, :], 0.0)
            link(V.memset(part[:, 2:3], float(DST_END)))
            for q in range(3):
                V.memset(ones96[32 * q:32 * q + 1, :], 1.0)
            dve.wait_ge(s_iota, 3)
            V.tensor_copy(enum[:, :], enum_i[:, :])
            V.tensor_copy(ramp[:, :], ramp_i[:, :])
            link(V.memset(part[:, 0:1], -1.0))
            link(V.tensor_copy(part[:, 1:2], part_i[:, :]))
            dve.wait_ge(s_rows, 64)
            V.tensor_copy(rows[:, 0, :], rows_i[:, 0, :])
            V.tensor_copy(rows[:, 1, :], rows_i[:, 1, :])
            link(V.tensor_scalar(tmp_i[:, :], rows_i[:, 0, :], 8, None, ALU.logical_shift_right))
            V.tensor_copy(rows[:, 2, :], tmp_i[:, :]).then_inc(s_padded, 1)
            dve.wait_ge(s_padded, 1)
            dve.wait_ge(s_pe, 1)
            link(V.tensor_copy(cols[:, 0:3, :], pX[:, 0:3 * T].rearrange("p (a t) -> p a t", a=3)))
            V.scalar_tensor_tensor(cols[:, 3, :], cols[:, 2, :], -float(LO), cols[:, 0, :], ALU.mult, ALU.add)
            V.tensor_scalar(idx[:, SRC_I, :], cols[:, 0, :], float(N - 1), None, ALU.min)
            link(V.tensor_scalar(idx[:, DST_I, :], cols[:, 1, :], float(N - 1), None, ALU.min))
            V.tensor_scalar(reach[:, :], cols[:, 0, :], float(LO - 1), 1.0, ALU.mult, ALU.add)
            V.memset(first_bc[:, 0:1], -1.0).then_inc(S("v_idx"), 1)
            dve.wait_ge(s_pe, 2)
            link(V.tensor_copy(first_bc[:, 1:T], pM[:, 0:T - 1]))
            V.tensor_copy(next_bc[:, 0:T - 1], pM[:, T + 1:2 * T])
            V.memset(next_bc[:, T - 1:T], -2.0)
            V.tensor_scalar(runs[:, 0, :], pM[0:T, 0:T], rows[:, 1, P - 1:P], None, ALU.is_equal)
            V.tensor_scalar(runs[:, 1, :], pM[0:T, T:2 * T], rows[:, 1, 0:1], None, ALU.is_equal
                            ).then_inc(S("v_runs"), 1)
            def one_hot(i):
                for k in range(BODY):
                    n, b = step(i, k), k % RING
                    wait(dve, s_hist, n - (RING - 1))
                    V.tensor_scalar(hot_hi[:, b, :], ramp[:, 0:HI], cols[:, 2, ds(n, 1)], None, ALU.is_equal)
                    V.tensor_scalar(hot_lo[:, b, :], ramp[:, :], cols[:, 3, ds(n, 1)], None, ALU.is_equal
                                    ).then_inc(s_hot, 1)
            run(dve, TURNS, one_hot)
            dve.wait_ge(s_pe, 3)
            V.tensor_copy(tab[:, :], pH[0:T, :]).then_inc(S("v_tab"), 1)
            dve.wait_ge(s_srt, 80)
            dve.wait_ge(s_pe, 4)
            link(V.tensor_copy(cols[:, 4, :], pX[:, 3 * T:4 * T]))
            link(V.tensor_tensor(fidx[:, 0, :], cols[:, 1, :], cols[:, 4, :], ALU.is_equal))
            link(V.scalar_tensor_tensor(idx[:, O_I, :], fidx[:, 0, :], 65536.0, cols[:, 1, :], ALU.mult, ALU.add))
            V.tensor_copy(before[:, :], srt[:, 0, 0:1])
            link(V.tensor_scalar(srt[:, 0, P + 1:P + 2], part[0:T, 1:2], float(P * LO), None, ALU.mult))
            link(V.tensor_scalar(srt[:, 1, P + 1:P + 2], srt[:, 0, P + 1:P + 2], -float(P * LO), 0.0,
                                 ALU.add, ALU.max))
            link(V.tensor_tensor(srt[:, 0, :], srt[:, 0, :], srt[:, 1, :], ALU.subtract))
            link(V.tensor_copy(srt_i[:, :], srt[:, 0, :]))
            link(V.tensor_scalar(srt_i[:, :], srt_i[:, :], 255, None, ALU.bitwise_and))
            link(V.tensor_copy(step_lo[:, :], srt_i[:, :]))
            link(V.tensor_tensor(step_hi[:, :], srt[:, 0, :], step_lo[:, :], ALU.subtract))
            dve.wait_ge(s_w, 16 * 17)
            link(V.tensor_scalar(eps1[:, :], eps1[:, :], 1.0, None, ALU.add))
            V.tensor_scalar(W1e[:, :], W1s[:, :], eps1[:, 0:1], None, ALU.mult)
            V.tensor_scalar(relu_cb[:, :, :], cb[:, :, :], 0.0, None, ALU.max).then_inc(s_ci, 1)
            link(V.tensor_copy(bhalf[:, :, :], braw[:, :, :]))
            for q in range(3):
                r_ = slice(32 * q, 32 * q + 1)
                V.tensor_copy(bsplit[r_, 0, :], bhalf[r_, 0, :])
                V.tensor_copy(bsplit[r_, 5:8, :], bhalf[r_, 2:5, :])
                link(V.tensor_copy(bsplit[r_, 1:5, :], bhalf[r_, 1, :].unsqueeze(1).to_broadcast([1, 4, D])))
                if q < 2:
                    link(V.tensor_tensor(braw[:, :, :], braw[:, :, :], bhalf[:, :, :], ALU.subtract))
                    link(V.tensor_copy(bhalf[:, :, :], braw[:, :, :]))
            V.memset(mark[:, :], 0.0).then_inc(S("v_bias"), 1)

            def chunk(i, a):
                dve.wait_ge(s_bc[a], i * 16 + (32 - 16 * a))
                wait(dve, s_look, i * BODY - BODY)
                V.tensor_scalar(above[a][:, :], src_bc[a], before[:, 0:1], None, ALU.is_ge).then_inc(s_hi, 1)
                V.tensor_tensor(cont[:, ds(i * CH, CH)].rearrange("p (t f) -> p t f", f=P),
                                dst_bc[a].rearrange("p (t f) -> p t f", f=P),
                                first_bc[:, ds(i * BODY, BODY)].unsqueeze(2).to_broadcast([P, BODY, P]), ALU.is_equal)
                for k in range(BODY):
                    n, b = step(i, k), k % LOOKS
                    last = V.tensor_scalar(same[:, ds(n * P, P)], dst_bc[a][:, k * P:(k + 1) * P], cols[:, 1, ds(n, 1)],
                                           None, ALU.is_equal, ALU.add, accum_out=own[:, ds(n, 1)])
                    if k == BODY - 1:
                        last.then_inc(s_bcused, 1)
                    dve.wait_ge(S("a_looked"), n + 1)
                    V.tensor_scalar(looked[b], looked[b], float(LO), look_banks[b][:, P + 1:P + 2],
                                    ALU.min, ALU.add, accum_out=found[:, ds(n, 1)]).then_inc(s_looked, 1)
            run_pairs(dve, chunk)
            dve.wait_ge(s_looked, T)
            dve.wait_ge(s_pe, 5)
            V.tensor_copy(ends[:, :, :], pS[0:T, 0:2 * P].rearrange("p (a m) -> p a m", a=2)).then_inc(S("v_ends"), 1)
            dve.wait_ge(s_pe, 6)
            V.tensor_tensor(deg_after[:, :], cols[:, 1, :], next_bc[:, :], ALU.is_equal)
            link(V.tensor_tensor(deg[:, :], cols[:, 1, :], first_bc[:, :], ALU.is_equal))
            V.tensor_tensor(deg_after[:, 0:T - 1], deg_after[:, 0:T - 1], pS[:, 2 * P + T + 1:2 * P + 2 * T], ALU.mult)
            link(V.tensor_tensor(deg[:, 1:T], deg[:, 1:T], pS[:, 2 * P:2 * P + T - 1], ALU.mult))
            link(V.tensor_tensor(deg[:, :], deg[:, :], own[:, :], ALU.add))
            link(V.tensor_tensor(deg[:, :], deg[:, :], deg_after[:, :], ALU.add))
            link(V.tensor_scalar(deg[:, :], deg[:, :], 1.0, None, ALU.max))
            link(V.tensor_copy(found_i[:, 0, :], found[:, :]))
            V.tensor_scalar(found_i[:, 1, :], found_i[:, 0, :], LO - 1, None, ALU.bitwise_and)
            link(V.tensor_scalar(found_i[:, 0, :], found_i[:, 0, :], 8, None, ALU.logical_shift_right))
            V.tensor_copy(below[:, :], found_i[:, 0, :])
            link(V.tensor_copy(equal[:, :], found_i[:, 1, :]))
            link(V.scalar_tensor_tensor(below[:, :], below[:, :], -1.0, equal[:, :], ALU.add, ALU.add))
            link(V.tensor_scalar(hit[:, :], equal[:, :], 1.0, None, ALU.min))
            link(V.tensor_scalar(fidx[:, 1, :], below[:, :], -float(EP + 1), None, ALU.add))
            link(V.tensor_tensor(fidx[:, 1, :], fidx[:, 1, :], hit[:, :], ALU.mult))
            link(V.tensor_scalar(idx[:, U_I, :], fidx[:, 1, :], float(EP), None, ALU.add))
            link(V.tensor_tensor(fidx[:, 0, :], below[:, :], enum[:, :], ALU.subtract))
            link(V.tensor_scalar(fidx[:, 0, :], fidx[:, 0, :], 2.0, -1.0, ALU.mult, ALU.add))
            link(V.tensor_tensor(fidx[:, 0, :], fidx[:, 0, :], hit[:, :], ALU.mult))
            link(V.scalar_tensor_tensor(idx[:, Y_I, :], enum[:, :], 2.0, fidx[:, 0, :], ALU.mult, ALU.add))
            V.memset(mark[:, :], 0.0).then_inc(S("v_rowidx"), 1)

            ahead(lambda g, stg, free: dense_dve(dve, g, stg))

            def scales():
                dve.wait_ge(S("g_counted"), 2 * TURNS)
                V.tensor_scalar(deg_out[:, :], deg_out[:, :], 1.0, None, ALU.max).then_inc(S("v_deg"), 1)
                dve.wait_ge(s_root, 1)
                V.reciprocal(deg[:, :], deg[:, :])
                link(V.reciprocal(deg_out[:, :], deg_out[:, :]))
                V.tensor_tensor(scale[:, :], deg[:, :], deg_out[:, :], ALU.mult).then_inc(S("v_scale"), 1)

            phase_loop(dve, "edge", "ahead", lambda i, k, stg: edge_dve(dve, i, k, stg),
                       lambda g, stg, free: dense_dve(dve, g, stg), scales)
            for c in (1, 2, 3):
                phase_loop(dve, f"conv{c}", PHASES[c - 1], lambda i, k, stg: conv_dve(dve, c, i, k, stg),
                           lambda g, stg, free: dense_dve(dve, g, stg))

        @block.scalar
        def _(act):
            act.wait_ge(S("v_idx"), 1)

            def look(i):
                for k in range(BODY):
                    n, b = step(i, k), k % LOOKS
                    act.wait_ge(s_look, n + 1)
                    wait(act, s_looked, n - lag(k))
                    nc.scalar.activation(looked[b], look_banks[b][:, 0:P + 1], ACT.Relu, scale=-float(LO - 1),
                                         bias=reach[:, ds(n, 1)]).then_inc(S("a_looked"), 1)
            run(act, TURNS, look)
            ahead(lambda g, stg, free: dense_act(act, g, stg))

            def roots():
                act.wait_ge(S("v_deg"), 1)
                nc.scalar.activation(deg[:, :], deg[:, :], ACT.Sqrt)
                nc.scalar.activation(deg_out[:, :], deg_out[:, :], ACT.Sqrt).then_inc(s_root, 1)
                act.wait_ge(S("v_scale"), 1)

            phase_loop(act, "edge", "ahead", lambda i, k, stg: edge_act(act, i, k, stg),
                       lambda g, stg, free: dense_act(act, g, stg), roots)
            for c in (1, 2, 3):
                phase_loop(act, f"conv{c}", PHASES[c - 1], lambda i, k, stg: conv_act(act, c, i, k, stg),
                           lambda g, stg, free: dense_act(act, g, stg))

        @block.tensor
        def _(pe):
            pe.wait_ge(s_iota, 3)
            pe.wait_ge(s_padded, 1)
            for a in range(3):
                last = nc.tensor.transpose(pX[:, a * T:(a + 1) * T], rows[:, a, :], ident[0:T, 0:T])
            last.then_inc(s_pe, 1)
            pe.wait_ge(S("v_idx"), 1)
            nc.tensor.matmul(pM[:, 0:T], last_row[:, :], cols[:, 1, :], start=True, stop=True)
            nc.tensor.matmul(pM[:, T:2 * T], first_row[:, :], cols[:, 1, :], start=True, stop=True).then_inc(s_pe, 1)
            nc.tensor.matmul(pH[0:T, :], zeros[:, 0:T], zeros[:, :], start=True, stop=False)

            def count(i):
                for k in range(BODY):
                    b = k % RING
                    pe.wait_ge(s_hot, step(i, k) + 1)
                    for a in range(2):
                        last = nc.tensor.matmul(pH[0:T, a * LO:(a + 1) * LO], hot_hi[:, b, a * T:(a + 1) * T],
                                                hot_lo[:, b, :], start=False, stop=False)
                    last.then_inc(s_hist, 1)
            run(pe, TURNS, count)
            nc.tensor.matmul(pH[0:T, :], zeros[:, 0:T], zeros[:, :], start=False, stop=True).then_inc(s_pe, 1)
            pe.wait_ge(s_srt, 80)
            nc.tensor.transpose(pX[:, 3 * T:4 * T], rows[:, 3, :], ident[0:T, 0:T]).then_inc(s_pe, 1)

            def look_up(i, a):
                pe.wait_ge(s_hi, i + 1)
                for k in range(BODY):
                    n, b = step(i, k), k % LOOKS
                    pc, cs = look_banks[b], slice(k * P, (k + 1) * P)
                    wait(pe, s_looked, n - lag(k))
                    nc.tensor.matmul(pc[:, 0:P + 2], above[a][:, cs], step_lo[:, :], start=True, stop=False)
                    nc.tensor.matmul(pc[:, 0:P + 2], above[a][:, cs], step_hi[:, :], start=False, stop=True
                                     ).then_inc(s_look, 1)
            run_pairs(pe, look_up)
            pe.wait_ge(s_bcused, TURNS)
            nc.tensor.matmul(pS[0:T, 0:P], own[:, :], last_row[:, :], start=True, stop=True)
            nc.tensor.matmul(pS[0:T, P:2 * P], own[:, :], first_row[:, :], start=True, stop=True).then_inc(s_pe, 1)
            pe.wait_ge(S("v_ends"), 1)
            pe.wait_ge(S("g_runs"), 1)
            for a in range(2):
                last = nc.tensor.matmul(pS[:, 2 * P + a * T:2 * P + (a + 1) * T], ends[:, a, :], runs[:, a, :],
                                        start=True, stop=True)
            last.then_inc(s_pe, 1)
            pe.wait_ge(S("v_bias"), 1)
            ahead(lambda g, stg, free: dense_pe(pe, g, stg))
            pe.wait_ge(S("v_rowidx"), 1)
            phase_loop(pe, "edge", "ahead", lambda i, k, stg: edge_pe(pe, i, k, stg),
                       lambda g, stg, free: dense_pe(pe, g, stg))
            for c in (1, 2, 3):
                phase_loop(pe, f"conv{c}", PHASES[c - 1], lambda i, k, stg: conv_pe(pe, c, i, k, stg),
                           lambda g, stg, free: dense_pe(pe, g, stg))


_INS = ["x", "src", "dst", "L0_gnn_W_edge", "L0_gnn_b_edge", "L0_gnn_W1", "L0_gnn_b1", "L0_gnn_W2", "L0_gnn_b2",
        "L0_gnn_eps", "L1_gnn_W1", "L1_gnn_b1", "L1_gnn_W2", "L1_gnn_b2", "L1_gnn_W3", "L1_gnn_b3"]


def kernel(**inputs):
    import numpy as _np
    import concourse.bacc as _bacc
    from concourse import mybir as _mybir
    from concourse.bass_utils import run_bass_kernel_spmd as _run

    nc = _bacc.Bacc("TRN2", target_bir_lowering=False, num_devices=1)
    arrays, args = {}, []
    for name in _INS:
        a = _np.ascontiguousarray(inputs[name])
        arrays[f"in_{name}"] = a
        args.append(nc.dram_tensor(f"in_{name}", a.shape, _mybir.dt.from_np(a.dtype), kind="ExternalInput").ap())
    args.append(nc.dram_tensor("out", (N, D), _mybir.dt.float32, kind="ExternalOutput").ap())
    build(nc, *args)
    r = _run(nc, [arrays], core_ids=[0])
    return r.results[0]["out"]
```
